# Optimizing a Trainium2 kernel written in Bass

```python
import numpy as np
import jax
import jax.numpy as jnp

def _softmax(x, axis=-1):
    return jax.nn.softmax(x, axis=axis)

def _gelu(x):
    return jax.nn.gelu(x, approximate=True)

def _silu(x):
    return jax.nn.silu(x)

def _sigmoid(x):
    return jax.nn.sigmoid(x)

def _layernorm(x, axis=-1, eps=1e-05):
    m = jnp.mean(x, axis=axis, keepdims=True)
    v = jnp.var(x, axis=axis, keepdims=True)
    return (x - m) / jnp.sqrt(v + eps)

def _scatter_add(tgt, idx, src, axis=0):
    return tgt.at[idx].add(src)

def _segment_sum(src, seg, n):
    return jax.ops.segment_sum(src, seg, n)
kernel_name = 'mk_conv_preact_d4_conv_nchw512_r4_a10635'

def setup_inputs(seed: int=0):
    np.random.seed(seed)
    _w = jnp.asarray

    def _rec_inputs():
        import jax
        import jax.numpy as jnp
        _gk = jax.random.key(seed)
        x = 7.22e-05 + 1 * jax.random.normal(jax.random.fold_in(_gk, 1), (4, 128, 16, 16), jnp.float32)
        return x
    x = _rec_inputs()

    def _L0_conv_setup():
        import jax, jax.numpy as jnp
        import numpy as np
        B, C, H, W = (4, 128, 16, 16)
        key = jax.random.key(seed)
        ks = jax.random.split(key, 9)
        s = 0.02
        return {'x': jax.random.normal(ks[0], (B, C, H, W), dtype=jnp.float32), 'Wq': jax.random.normal(ks[1], (C, C), dtype=jnp.float32) * s, 'bq': jnp.zeros((C,), dtype=jnp.float32), 'Wk': jax.random.normal(ks[2], (C, C), dtype=jnp.float32) * s, 'bk': jnp.zeros((C,), dtype=jnp.float32), 'Wv': jax.random.normal(ks[3], (C, C), dtype=jnp.float32) * s, 'bv': jnp.zeros((C,), dtype=jnp.float32), 'Wo': jax.random.normal(ks[4], (C, C), dtype=jnp.float32) * s, 'bo': jnp.zeros((C,), dtype=jnp.float32)}
    _L0_conv_all = _L0_conv_setup()
    _L0_conv_in = {k: v for k, v in _L0_conv_all.items() if k in ('Wq', 'bq', 'Wk', 'bk', 'Wv', 'bv', 'Wo', 'bo')}
    del _L0_conv_all

    def _L1_conv_setup():
        import jax, jax.numpy as jnp
        import numpy as np
        from jax import lax
        EPS = 1e-05
        GROUPS = 16

        def _batchnorm(x, gamma, beta):
            m = jnp.mean(x, axis=(0, 2, 3), keepdims=True)
            v = jnp.mean((x - m) ** 2, axis=(0, 2, 3), keepdims=True)
            xhat = (x - m) * lax.rsqrt(v + EPS)
            return xhat * gamma[None, :, None, None] + beta[None, :, None, None]

        @jax.custom_vjp
        def binary_act(x):
            return jnp.sign(x)

        def _ba_fwd(x):
            return (jnp.sign(x), x)

        def _ba_bwd(x, g):
            return (jnp.clip(2.0 - 2.0 * jnp.abs(x), a_min=0.0) * g,)
        binary_act.defvjp(_ba_fwd, _ba_bwd)

        @jax.custom_vjp
        def binary_weight(w):
            return jnp.sign(w)

        def _bw_fwd(w):
            return (jnp.sign(w), w)

        def _bw_bwd(w, g):
            mask = jnp.logical_or(w >= 1.0, w <= -1.0)
            return (jnp.where(mask, 0.0, g),)
        binary_weight.defvjp(_bw_fwd, _bw_bwd)

        def _weight_scale(w):
            co = w.shape[0]
            wf = w.reshape(co, -1)
            bw = wf - jnp.mean(wf, axis=-1, keepdims=True)
            std = jnp.std(wf - jnp.mean(wf, axis=-1, keepdims=True), axis=-1, ddof=1, keepdims=True)
            bw = bw / std
            sw = jnp.mean(jnp.abs(bw), axis=-1).reshape(co, 1, 1, 1)
            return lax.stop_gradient(sw)
        key = jax.random.key(seed)
        ks = jax.random.split(key, 7)
        N, C, H, W = (16, 128, 32, 32)
        k = 3
        x = jax.random.normal(ks[0], (N, C, H, W), dtype=jnp.float32)
        conv_w = jax.random.normal(ks[1], (C, C // GROUPS, k, k), dtype=jnp.float32) * 0.1
        bn1_gamma = jnp.ones((C,), jnp.float32)
        bn1_beta = jnp.zeros((C,), jnp.float32)
        bn2_gamma = jnp.ones((C,), jnp.float32)
        bn2_beta = jnp.zeros((C,), jnp.float32)
        prelu_a = jnp.full((C,), 0.25, jnp.float32)
        return {'x': x, 'conv_w': conv_w, 'bn1_gamma': bn1_gamma, 'bn1_beta': bn1_beta, 'bn2_gamma': bn2_gamma, 'bn2_beta': bn2_beta, 'prelu_a': prelu_a}
    _L1_conv_all = _L1_conv_setup()
    _L1_conv_in = {k: v for k, v in _L1_conv_all.items() if k in ('conv_w', 'bn1_gamma', 'bn1_beta', 'bn2_gamma', 'bn2_beta', 'prelu_a')}
    del _L1_conv_all

    def _L2_conv_setup():
        import jax, jax.numpy as jnp
        import numpy as np
        from jax import lax
        EPS = 1e-05
        DW_THRESH = 4.0
        PW_THRESH = 0.001
        C_IN = 128
        C_OUT = 128

        def _bn(x, g, b, m, v):
            inv = g * lax.rsqrt(v + EPS)
            return x * inv[None, :, None, None] + (b - m * inv)[None, :, None, None]

        def _prune(x, thresh):
            amax = jnp.max(jnp.abs(x), axis=(2, 3), keepdims=True)
            return jnp.where(amax < thresh, jnp.zeros_like(x), x)
        key = jax.random.key(seed)
        ks = jax.random.split(key, 8)
        B, H, W = (16, 28, 28)
        x = jax.random.normal(ks[0], (B, C_IN, H, W), dtype=jnp.float32)
        dw_w = jax.random.normal(ks[1], (C_IN, 1, 3, 3), dtype=jnp.float32) * 0.1
        dw_b = jax.random.normal(ks[2], (C_IN,), dtype=jnp.float32) * 0.1
        bn1_g = jnp.ones((C_IN,), jnp.float32)
        bn1_b = jnp.zeros((C_IN,), jnp.float32)
        bn1_m = jnp.zeros((C_IN,), jnp.float32)
        bn1_v = jnp.ones((C_IN,), jnp.float32)
        pw_w = jax.random.normal(ks[3], (C_OUT, C_IN, 1, 1), dtype=jnp.float32) * 0.05
        pw_b = jax.random.normal(ks[4], (C_OUT,), dtype=jnp.float32) * 0.1
        bn2_g = jnp.ones((C_OUT,), jnp.float32)
        bn2_b = jnp.zeros((C_OUT,), jnp.float32)
        bn2_m = jnp.zeros((C_OUT,), jnp.float32)
        bn2_v = jnp.ones((C_OUT,), jnp.float32)
        return dict(x=x, dw_w=dw_w, dw_b=dw_b, bn1_g=bn1_g, bn1_b=bn1_b, bn1_m=bn1_m, bn1_v=bn1_v, pw_w=pw_w, pw_b=pw_b, bn2_g=bn2_g, bn2_b=bn2_b, bn2_m=bn2_m, bn2_v=bn2_v)
    _L2_conv_all = _L2_conv_setup()
    _L2_conv_in = {k: v for k, v in _L2_conv_all.items() if k in ('dw_w', 'dw_b', 'bn1_g', 'bn1_b', 'bn1_m', 'bn1_v', 'pw_w', 'pw_b', 'bn2_g', 'bn2_b', 'bn2_m', 'bn2_v')}
    del _L2_conv_all

    def _L3_conv_setup():
        import jax, jax.numpy as jnp
        import numpy as np
        HEADS = 8
        DIM_HEAD = 16
        key = jax.random.key(seed)
        k1, k2, k3 = jax.random.split(key, 3)
        dim = 128
        hidden = HEADS * DIM_HEAD
        x = jax.random.normal(k1, (16, dim, 16, 16), dtype=jnp.float32)
        w_qkv = jax.random.normal(k2, (3 * hidden, dim), dtype=jnp.float32) * (1.0 / np.sqrt(dim))
        w_out = jax.random.normal(k3, (dim, hidden), dtype=jnp.float32) * (1.0 / np.sqrt(hidden))
        b_out = jnp.zeros((dim,), dtype=jnp.float32)
        return {'x': x, 'w_qkv': w_qkv, 'w_out': w_out, 'b_out': b_out}
    _L3_conv_all = _L3_conv_setup()
    _L3_conv_in = {k: v for k, v in _L3_conv_all.items() if k in ('w_qkv', 'w_out', 'b_out')}
    del _L3_conv_all
    return {'x': x, 'L0_conv_Wq': _L0_conv_in['Wq'], 'L0_conv_bq': _L0_conv_in['bq'], 'L0_conv_Wk': _L0_conv_in['Wk'], 'L0_conv_bk': _L0_conv_in['bk'], 'L0_conv_Wv': _L0_conv_in['Wv'], 'L0_conv_bv': _L0_conv_in['bv'], 'L0_conv_Wo': _L0_conv_in['Wo'], 'L0_conv_bo': _L0_conv_in['bo'], 'L1_conv_conv_w': _L1_conv_in['conv_w'], 'L1_conv_bn1_gamma': _L1_conv_in['bn1_gamma'], 'L1_conv_bn1_beta': _L1_conv_in['bn1_beta'], 'L1_conv_bn2_gamma': _L1_conv_in['bn2_gamma'], 'L1_conv_bn2_beta': _L1_conv_in['bn2_beta'], 'L1_conv_prelu_a': _L1_conv_in['prelu_a'], 'L2_conv_dw_w': _L2_conv_in['dw_w'], 'L2_conv_dw_b': _L2_conv_in['dw_b'], 'L2_conv_bn1_g': _L2_conv_in['bn1_g'], 'L2_conv_bn1_b': _L2_conv_in['bn1_b'], 'L2_conv_bn1_m': _L2_conv_in['bn1_m'], 'L2_conv_bn1_v': _L2_conv_in['bn1_v'], 'L2_conv_pw_w': _L2_conv_in['pw_w'], 'L2_conv_pw_b': _L2_conv_in['pw_b'], 'L2_conv_bn2_g': _L2_conv_in['bn2_g'], 'L2_conv_bn2_b': _L2_conv_in['bn2_b'], 'L2_conv_bn2_m': _L2_conv_in['bn2_m'], 'L2_conv_bn2_v': _L2_conv_in['bn2_v'], 'L3_conv_w_qkv': _L3_conv_in['w_qkv'], 'L3_conv_w_out': _L3_conv_in['w_out'], 'L3_conv_b_out': _L3_conv_in['b_out']}

def reference(x, L0_conv_Wq, L0_conv_bq, L0_conv_Wk, L0_conv_bk, L0_conv_Wv, L0_conv_bv, L0_conv_Wo, L0_conv_bo, L1_conv_conv_w, L1_conv_bn1_gamma, L1_conv_bn1_beta, L1_conv_bn2_gamma, L1_conv_bn2_beta, L1_conv_prelu_a, L2_conv_dw_w, L2_conv_dw_b, L2_conv_bn1_g, L2_conv_bn1_b, L2_conv_bn1_m, L2_conv_bn1_v, L2_conv_pw_w, L2_conv_pw_b, L2_conv_bn2_g, L2_conv_bn2_b, L2_conv_bn2_m, L2_conv_bn2_v, L3_conv_w_qkv, L3_conv_w_out, L3_conv_b_out):
    import jax
    import jax.numpy as jnp

    def _L0_conv_ref(x, Wq, bq, Wk, bk, Wv, bv, Wo, bo):
        import jax, jax.numpy as jnp
        import numpy as np
        B, C, H, W = (4, 128, 16, 16)
        b, c, h, w = x.shape
        t = jnp.swapaxes(x.reshape(b, c, h * w), 1, 2)
        q = t @ Wq.T + bq
        k = t @ Wk.T + bk
        v = t @ Wv.T + bv
        scale = 1.0 / jnp.sqrt(jnp.asarray(c, dtype=t.dtype))
        scores = jnp.einsum('bnc,bmc->bnm', q, k) * scale
        attn = jax.nn.softmax(scores, axis=-1)
        out = jnp.einsum('bnm,bmc->bnc', attn, v)
        out = out @ Wo.T + bo
        return out.reshape(b, c, h, w)

    def _L1_conv_ref(x, conv_w, bn1_gamma, bn1_beta, bn2_gamma, bn2_beta, prelu_a):
        import jax, jax.numpy as jnp
        import numpy as np
        from jax import lax
        EPS = 1e-05
        GROUPS = 16

        def _batchnorm(x, gamma, beta):
            m = jnp.mean(x, axis=(0, 2, 3), keepdims=True)
            v = jnp.mean((x - m) ** 2, axis=(0, 2, 3), keepdims=True)
            xhat = (x - m) * lax.rsqrt(v + EPS)
            return xhat * gamma[None, :, None, None] + beta[None, :, None, None]

        @jax.custom_vjp
        def binary_act(x):
            return jnp.sign(x)

        def _ba_fwd(x):
            return (jnp.sign(x), x)

        def _ba_bwd(x, g):
            return (jnp.clip(2.0 - 2.0 * jnp.abs(x), a_min=0.0) * g,)
        binary_act.defvjp(_ba_fwd, _ba_bwd)

        @jax.custom_vjp
        def binary_weight(w):
            return jnp.sign(w)

        def _bw_fwd(w):
            return (jnp.sign(w), w)

        def _bw_bwd(w, g):
            mask = jnp.logical_or(w >= 1.0, w <= -1.0)
            return (jnp.where(mask, 0.0, g),)
        binary_weight.defvjp(_bw_fwd, _bw_bwd)

        def _weight_scale(w):
            co = w.shape[0]
            wf = w.reshape(co, -1)
            bw = wf - jnp.mean(wf, axis=-1, keepdims=True)
            std = jnp.std(wf - jnp.mean(wf, axis=-1, keepdims=True), axis=-1, ddof=1, keepdims=True)
            bw = bw / std
            sw = jnp.mean(jnp.abs(bw), axis=-1).reshape(co, 1, 1, 1)
            return lax.stop_gradient(sw)
        res = x
        h = _batchnorm(x, bn1_gamma, bn1_beta)
        h = binary_act(h)
        sw = _weight_scale(conv_w)
        bw = binary_weight(conv_w) * sw
        h = lax.conv_general_dilated(h, bw, window_strides=(1, 1), padding=((1, 1), (1, 1)), feature_group_count=GROUPS, dimension_numbers=('NCHW', 'OIHW', 'NCHW'))
        h = _batchnorm(h, bn2_gamma, bn2_beta)
        h = h + res
        a = prelu_a[None, :, None, None]
        return jnp.where(h > 0, h, a * h)

    def _L2_conv_ref(x, dw_w, dw_b, bn1_g, bn1_b, bn1_m, bn1_v, pw_w, pw_b, bn2_g, bn2_b, bn2_m, bn2_v):
        import jax, jax.numpy as jnp
        import numpy as np
        from jax import lax
        EPS = 1e-05
        DW_THRESH = 4.0
        PW_THRESH = 0.001
        C_IN = 128
        C_OUT = 128

        def _bn(x, g, b, m, v):
            inv = g * lax.rsqrt(v + EPS)
            return x * inv[None, :, None, None] + (b - m * inv)[None, :, None, None]

        def _prune(x, thresh):
            amax = jnp.max(jnp.abs(x), axis=(2, 3), keepdims=True)
            return jnp.where(amax < thresh, jnp.zeros_like(x), x)
        dn = ('NCHW', 'OIHW', 'NCHW')
        h = lax.conv_general_dilated(x, dw_w, window_strides=(1, 1), padding=((1, 1), (1, 1)), feature_group_count=C_IN, dimension_numbers=dn)
        h = h + dw_b[None, :, None, None]
        h = jax.nn.relu(_bn(h, bn1_g, bn1_b, bn1_m, bn1_v))
        h = _prune(h, DW_THRESH)
        h = lax.conv_general_dilated(h, pw_w, window_strides=(1, 1), padding=((0, 0), (0, 0)), dimension_numbers=dn)
        h = h + pw_b[None, :, None, None]
        h = jax.nn.relu(_bn(h, bn2_g, bn2_b, bn2_m, bn2_v))
        h = _prune(h, PW_THRESH)
        return h

    def _L3_conv_ref(x, w_qkv, w_out, b_out):
        import jax, jax.numpy as jnp
        import numpy as np
        HEADS = 8
        DIM_HEAD = 16
        b, c, h, w = x.shape
        n = h * w
        xf = x.reshape(b, c, n)
        qkv = jnp.einsum('oc,bcn->bon', w_qkv, xf)
        qkv = qkv.reshape(b, 3, HEADS, DIM_HEAD, n)
        q, k, v = (qkv[:, 0], qkv[:, 1], qkv[:, 2])
        k = jax.nn.softmax(k, axis=-1)
        context = jnp.einsum('bhdn,bhen->bhde', k, v)
        out = jnp.einsum('bhde,bhdn->bhen', context, q)
        out = out.reshape(b, HEADS * DIM_HEAD, n)
        out = jnp.einsum('oc,bcn->bon', w_out, out) + b_out[None, :, None]
        return out.reshape(b, -1, h, w)

    def _gn(v, G=32, eps=1e-05):
        B_, C_, H_, W_ = v.shape
        g = v.reshape(B_, G, C_ // G, H_, W_)
        m = jnp.mean(g, axis=(2, 3, 4), keepdims=True)
        s = jnp.var(g, axis=(2, 3, 4), keepdims=True)
        return ((g - m) / jnp.sqrt(s + eps)).reshape(v.shape)

    def _ln_c(v, eps=1e-06):
        m = jnp.mean(v, axis=1, keepdims=True)
        s = jnp.var(v, axis=1, keepdims=True)
        return (v - m) / jnp.sqrt(s + eps)

    def _ln_t(v, eps=1e-05):
        m = jnp.mean(v, axis=-1, keepdims=True)
        s = jnp.var(v, axis=-1, keepdims=True)
        return (v - m) / jnp.sqrt(s + eps)

    def _to_tokens(v):
        B_, C_, H_, W_ = v.shape
        return v.reshape(B_, C_, H_ * W_).transpose(0, 2, 1)

    def _from_tokens(t, like):
        B_, C_, H_, W_ = like.shape
        return t.transpose(0, 2, 1).reshape(B_, C_, H_, W_)
    x = x + _L0_conv_ref(_gn(x), L0_conv_Wq, L0_conv_bq, L0_conv_Wk, L0_conv_bk, L0_conv_Wv, L0_conv_bv, L0_conv_Wo, L0_conv_bo)
    x = x + _L1_conv_ref(_gn(x), L1_conv_conv_w, L1_conv_bn1_gamma, L1_conv_bn1_beta, L1_conv_bn2_gamma, L1_conv_bn2_beta, L1_conv_prelu_a)
    x = x + _L2_conv_ref(_gn(x), L2_conv_dw_w, L2_conv_dw_b, L2_conv_bn1_g, L2_conv_bn1_b, L2_conv_bn1_m, L2_conv_bn1_v, L2_conv_pw_w, L2_conv_pw_b, L2_conv_bn2_g, L2_conv_bn2_b, L2_conv_bn2_m, L2_conv_bn2_v)
    x = x + _L3_conv_ref(_gn(x), L3_conv_w_qkv, L3_conv_w_out, L3_conv_b_out)
    return x

_drawn_inputs = setup_inputs


def setup_inputs(seed=0):
    import zlib

    import numpy as np

    out = dict(_drawn_inputs(seed))
    spreads = {'L0_conv_bq': (0.0, 0.8),
     'L0_conv_bk': (0.0, 0.8),
     'L0_conv_bv': (0.0, 0.1),
     'L0_conv_bo': (0.0, 0.1),
     'L1_conv_bn1_gamma': (1.0, 0.2),
     'L1_conv_bn1_beta': (0.0, 0.1),
     'L1_conv_bn2_gamma': (1.0, 0.2),
     'L1_conv_bn2_beta': (0.0, 0.1),
     'L1_conv_prelu_a': (0.25, 0.2),
     'L2_conv_bn1_g': (1.0, 0.2),
     'L2_conv_bn1_b': (0.0, 0.1),
     'L2_conv_bn1_m': (0.0, 0.1),
     'L2_conv_bn1_v': (1.0, 0.2),
     'L2_conv_bn2_g': (1.0, 0.6),
     'L2_conv_bn2_b': (0.0, 0.1),
     'L2_conv_bn2_m': (0.0, 0.1),
     'L2_conv_bn2_v': (1.0, 0.6),
     'L3_conv_b_out': (0.0, 0.1)}
    factors = {'L0_conv_Wq': 8.0, 'L0_conv_Wk': 7.677, 'L0_conv_Wv': 2.834}
    for name, (base, spread) in spreads.items():
        noise = np.random.default_rng([zlib.crc32(name.encode()), seed]).standard_normal(out[name].shape)
        drawn = base * np.exp(spread * noise) if base else spread * noise
        out[name] = jnp.asarray(drawn.astype(out[name].dtype))
    for name, factor in factors.items():
        out[name] = (out[name] * factor).astype(out[name].dtype)
    return out
```

```python
import concourse.bass as bass
from concourse import mybir
from contextlib import ExitStack

B, C, H, W = 4, 128, 16, 16
N = H * W
HALF = N // 2
TAPS = 9
PH, PW = H + 2, W + 2
GN_GROUP = C // 32
CONV_GROUP = C // 16
HEAD = 16
CONV_FAN = CONV_GROUP * TAPS
EPS = 1e-5
DW_THRESH = 4.0
PW_THRESH = 0.001

EARLY = [("wqT", C), ("wkT", C), ("wv", C), ("woT", C), ("bq", 1), ("bk", 1), ("bv", 1), ("bo", 1)]
LATE = [("conv_in", TAPS * CONV_GROUP), ("conv_out", CONV_FAN), ("dw", TAPS),
        ("bn1_gamma", 1), ("bn1_beta", 1), ("bn2_gamma", 1), ("bn2_beta", 1), ("prelu", 1),
        ("l2_bias", 2), ("l2_g", 2), ("l2_b", 2), ("l2_m", 2), ("l2_v", 2), ("b_out", 1),
        ("pwT", C), ("wqkvT", 3 * C), ("woutT", C)]


def columns(fields):
    at, out = 0, {}
    for name, width in fields:
        out[name] = slice(at, at + width)
        at += width
    return out, at


def build(nc, x, early, late, out):
    fp32, bf16 = mybir.dt.float32, mybir.dt.bfloat16
    ALU = mybir.AluOpType
    ACT = mybir.ActivationFunctionType
    X_AXIS = mybir.AxisListType.X
    EC, EARLY_W = columns(EARLY)
    LC, LATE_W = columns(LATE)
    x_v = x.rearrange("b c h w -> b c (h w)")
    out_v = out.rearrange("b c h w -> b c (h w)")

    ctx = ExitStack()
    with ctx:
        def sb(name, shape, dt=fp32):
            return ctx.enter_context(nc.sbuf_tensor(name, shape, dt))

        def sem(name):
            return ctx.enter_context(nc.semaphore(name))

        ep = sb("early_params", [C, EARLY_W])
        lp = sb("late_params", [C, LATE_W])
        ident = sb("ident", [C, C])
        ones = sb("ones", [C, C])
        group_avg = sb("group_avg", [C, C])
        head_mask = sb("head_mask", [C, C])
        conv_mask = sb("conv_mask", [C, C // CONV_GROUP], bf16)
        eps_rhs = sb("eps_rhs", [C, 2])
        minus_half = sb("minus_half", [C, B])
        bias_rows = sb("bias_rows", [C, 2, C])
        setup = sb("setup", [C, 2, C])
        woT_v = setup[:, 0, :]
        v_bias = setup[:, 1, :]
        bq_s = sb("bq_scaled", [C, 1])
        conv_sign = sb("conv_sign", [C, TAPS, CONV_GROUP], bf16)
        conv_w = sb("conv_blocks", [C, TAPS, C], bf16)
        dw_diag = sb("dw_diag", [C, TAPS, C])
        sw_st = sb("sw_stats", [C, 6])
        sw_mv = sb("sw_mean_var", [C, 2])
        sw_dev = sb("sw_deviation", [C, CONV_FAN])
        sw_abs = sb("sw_abs_sum", [C, 1])
        sw_var = sb("sw_var", [C, 1])
        sw_rstd = sb("sw_rstd", [C, 1])
        sw = sb("sw", [C, 1])
        sw_sq = sb("sw_squared", [C, 1])
        sw_gamma = sb("sw_gamma", [C, 1])
        l2_ve = sb("l2_var_eps", [C, 2])
        l2_rs = sb("l2_rstd", [C, 2])
        l2_scale = sb("l2_scale", [C, 2])
        l2_t = sb("l2_t", [C, 2])
        l2_t2 = sb("l2_t2", [C, 2])
        l2_shift = sb("l2_shift", [C, 2])

        xs = [sb(f"x{i}", [C, B, N]) for i in range(5)]
        t0 = sb("t0", [C, B, N])
        res = sb("res", [C, B, N])
        pad2 = sb("pad2", [C, B, PH, PW])
        t3 = sb("t3", [C, B, N])
        signs = sb("signs", [C, B, PH, PW], bf16)
        q = sb("q", [C, B, N])
        k = sb("k", [C, B, N])
        vt = sb("vt", [C, B, 2, C])
        nmax = sb("nmax", [C, B, 2])
        prob = sb("prob", [C, B, 2, N])
        psum_rows = sb("prob_sum", [C, B, 2])
        rinv = sb("rinv", [C, B, 2])
        probT = sb("probT", [C, B, 2, 2, C])
        x1_res = sb("x1_res", [C, B, N])
        bn2_out = sb("bn2_out", [C, B, N])
        h1 = sb("h1", [C, B, N])
        x1_h1 = sb("x1_h1", [C, B, N])
        h1_neg = sb("h1_neg", [C, B, N])
        one_minus_a = sb("one_minus_a", [C, 1])
        h2 = sb("h2", [C, B, N])
        amax = sb("amax", [C, B, 2])
        keep = sb("keep", [C, B, 2])
        pwT_kept = sb("pwT_kept", [C, B, C])
        y2 = sb("y2", [C, B, N])
        q3 = sb("q3", [C, B, N])
        nmax3 = sb("nmax3", [C, B])
        e3 = sb("e3", [C, B, N])
        sum3 = sb("sum3", [C, B])
        rinv3 = sb("rinv3", [C, B])
        vt3 = sb("vt3", [C, B, 2, C])
        kt3 = sb("kt3", [C, B, 2, C])
        ctxT = sb("ctxT", [C, B, C])
        proj = sb("proj", [C, B, C])

        st = sb("gn_stats", [C, 4, B, 6])
        mv = sb("gn_mean_sq", [C, 4, B, 2])
        gs = sb("gn_group", [C, 4, B, 2])
        ve = sb("gn_var_eps", [C, 4, B])
        rstd = sb("gn_rstd", [C, 4, B])
        bn_mv = sb("bn_mean_var", [C, 2, 2])
        bn_ve = sb("bn_var_eps", [C, 2])
        bn_rs = sb("bn_rstd", [C, 2])
        bn_scale = sb("bn_scale", [C, 2])
        bn_t = sb("bn_t", [C, 2])
        bn_shift = sb("bn_shift", [C, 2])
        bn2_st = sb("bn2_stats", [C, B, 6])

        banks = [ctx.enter_context(nc.psum_tensor(f"bank{i}", [C, 512], fp32)) for i in range(8)]

        q_ps, k_ps = banks[0][:, 0:N], banks[1][:, 0:N]
        v_ps = banks[2][:, 0:N]
        s_ps = [banks[3], banks[4]]
        pt_ps = banks[5]
        o_ps = banks[6][:, 0:N]
        setup_ps = banks[6]
        conv_ps = [banks[i][:, 0:N] for i in (0, 1, 2, 5)]
        dw_ps = [banks[3 + b % 2][:, 0:N] for b in range(B)]
        pw_ps = [banks[(6, 2)[b % 2]][:, 0:N] for b in range(B)]
        kt_ps = banks[3][:, 0:N]
        cx_ps, pj_ps = banks[4][:, 0:C], banks[4][:, C:2 * C]
        vt_ps = banks[5][:, 0:N]
        gn_ps = banks[7][:, 0:2]

        x_in = [sem(f"x_in{b}") for b in range(B)]
        early_in = sem("early_in")
        late_in = sem("late_in")
        stored = sem("stored")
        pool_step = sem("pool_step")
        gn_consts = sem("gn_consts")
        pool_consts = sem("pool_consts")
        mask_ready = sem("mask_ready")
        conv_w_ready = sem("conv_w_ready")
        dw_diag_ready = sem("dw_diag_ready")
        l2_consts = sem("l2_consts")
        borders = sem("borders")
        conv_sign_ready = sem("conv_sign_ready")
        setup_mm = sem("setup_mm")
        setup_done = sem("setup_done")
        dve_step = sem("dve_step")
        stats_ready = sem("stats_ready")
        group_ready = sem("group_ready")
        group_out = sem("group_out")
        var_ready = sem("var_ready")
        rstd_ready = sem("rstd_ready")
        t_ready = [sem(f"t_ready{i}") for i in range(4)]
        q_mm = sem("q_mm")
        k_mm = sem("k_mm")
        v_mm = sem("v_mm")
        q_ready = sem("q_ready")
        k_ready = sem("k_ready")
        v_ready = sem("v_ready")
        s_mm = sem("s_mm")
        nmax_ready = sem("nmax_ready")
        exp_ready = sem("exp_ready")
        pt_mm = sem("pt_mm")
        pt_ready = sem("pt_ready")
        o_mm = sem("o_mm")
        x1_ready = sem("x1_ready")
        bn1_ready = sem("bn1_ready")
        sign_ready = sem("sign_ready")
        conv_mm = sem("conv_mm")
        bn2_out_ready = sem("bn2_out_ready")
        h1_ready = sem("h1_ready")
        h1_neg_ready = sem("h1_neg_ready")
        x1_h1_ready = sem("x1_h1_ready")
        bn2_shift_ready = sem("bn2_shift_ready")
        dw_mm = sem("dw_mm")
        h2_ready = sem("h2_ready")
        pwT_ready = sem("pwT_ready")
        pw_mm = sem("pw_mm")
        y2_ready = sem("y2_ready")
        q3_mm = sem("q3_mm")
        k3_mm = sem("k3_mm")
        vt3_mm = sem("vt3_mm")
        nmax3_ready = sem("nmax3_ready")
        q3_ready = sem("q3_ready")
        e3_ready = sem("e3_ready")
        vt3_ready = sem("vt3_ready")
        kt3_mm = sem("kt3_mm")
        kt3_ready = sem("kt3_ready")
        cx_mm = sem("cx_mm")
        cx_ready = sem("cx_ready")
        pj_mm = sem("pj_mm")
        pj_ready = sem("pj_ready")
        y3_mm = sem("y3_mm")
        x4_ready = sem("x4_ready")

        SCALE = float(C) ** -0.5
        ROOTS = [("gn", 0, b) for b in range(B)] + [("sw",)] + [("gn", 1, b) for b in range(B)] \
            + [("bn", 0), ("bn", 1)] + [("gn", layer, b) for layer in (2, 3) for b in range(B)]

        def root(*what):
            return ROOTS.index(what) + 1

        block = ctx.enter_context(nc.Block())

        @block.sync
        def _(sp):
            for b in range(B):
                sp.dma_start(xs[0][:, b, :], x_v[b]).then_inc(x_in[b], 16)
            sp.dma_start(lp[:, :], late).then_inc(late_in, 16)
            for b in range(B):
                sp.wait_ge(x4_ready, b + 1)
                sp.dma_start(out_v[b], xs[4][:, b, :]).then_inc(stored, 16)
            sp.wait_ge(stored, 16 * B)

        @block.gpsimd
        def _(pool):
            steps = [0]

            def step(ins):
                steps[0] += 1
                ins.then_inc(pool_step, 1)
                pool.wait_ge(pool_step, steps[0])

            def same_block(tile, size):
                inner = [[0, size]] if tile.shape[1] == C else []
                step(nc.gpsimd.affine_select(out=tile[:, :], in_=tile[:, :], compare_op=ALU.is_ge,
                                             fill=0.0, base=0, pattern=[[-size, C // size]] + inner,
                                             channel_multiplier=1))
                return nc.gpsimd.affine_select(out=tile[:, :], in_=tile[:, :], compare_op=ALU.is_ge,
                                               fill=0.0, base=size - 1,
                                               pattern=[[size, C // size]] + inner,
                                               channel_multiplier=-1)

            nc.gpsimd.memset(ones[:, :], 1.0)
            nc.gpsimd.memset(eps_rhs[:, 0:1], 0.0)
            nc.gpsimd.memset(eps_rhs[:, 1:2], EPS / C)
            nc.gpsimd.memset(minus_half[:, :], -0.5)
            step(nc.gpsimd.memset(group_avg[:, :], 1.0 / GN_GROUP))
            same_block(group_avg, GN_GROUP).then_inc(gn_consts, 1)
            step(nc.gpsimd.memset(ident[:, :], 0.0))
            nc.gpsimd.affine_select(out=ident[:, :], in_=ident[:, :], compare_op=ALU.not_equal,
                                    fill=1.0, base=0, pattern=[[-1, C]],
                                    channel_multiplier=1).then_inc(pool_consts, 1)
            pool.wait_ge(early_in, 16)
            for i, name in enumerate(("bv", "bo")):
                ins = nc.gpsimd.tensor_scalar(bias_rows[:, i, :], ones[:, :], ep[:, EC[name]], 0.0,
                                              ALU.mult, ALU.add)
            ins.then_inc(pool_consts, 1)

            def roots(out_ap, in_ap, n, *what):
                pool.wait_ge(var_ready, root(*what))
                nc.gpsimd.tensor_tensor(out_ap, in_ap, minus_half[:, 0:n],
                                        ALU.pow).then_inc(rstd_ready, 1)

            for b in range(B):
                roots(rstd[:, 0, b:b + 1], ve[:, 0, b:b + 1], 1, "gn", 0, b)

            step(nc.gpsimd.memset(conv_mask[:, :], 1.0))
            step(same_block(conv_mask, CONV_GROUP))
            pool.wait_ge(conv_sign_ready, 1)
            groups = C // CONV_GROUP
            for tap in range(TAPS):
                ins = nc.gpsimd.tensor_tensor(
                    conv_w[:, tap, :].rearrange("p (g o) -> p g o", o=CONV_GROUP),
                    conv_sign[:, tap, :].unsqueeze(1).to_broadcast([C, groups, CONV_GROUP]),
                    conv_mask[:, :].unsqueeze(2).to_broadcast([C, groups, CONV_GROUP]), ALU.mult)
            ins.then_inc(conv_w_ready, 1)
            roots(sw_rstd[:, :], sw_var[:, :], 1, "sw")
            step(nc.gpsimd.tensor_scalar(l2_ve[:, :], lp[:, LC["l2_v"]], 1.0, EPS, ALU.mult, ALU.add))
            step(nc.gpsimd.tensor_tensor(l2_rs[:, :], l2_ve[:, :], minus_half[:, 0:2], ALU.pow))
            nc.gpsimd.tensor_tensor(l2_t[:, :], lp[:, LC["l2_bias"]], lp[:, LC["l2_m"]], ALU.subtract)
            step(nc.gpsimd.tensor_tensor(l2_scale[:, :], l2_rs[:, :], lp[:, LC["l2_g"]], ALU.mult))
            step(nc.gpsimd.tensor_tensor(l2_t2[:, :], l2_t[:, :], l2_scale[:, :], ALU.mult))
            nc.gpsimd.tensor_tensor(l2_shift[:, :], l2_t2[:, :], lp[:, LC["l2_b"]],
                                    ALU.add).then_inc(l2_consts, 1)
            for tap in range(TAPS):
                ins = nc.gpsimd.tensor_scalar(dw_diag[:, tap, :], ident[:, :],
                                              lp[:, LC["dw"].start + tap:LC["dw"].start + tap + 1],
                                              0.0, ALU.mult, ALU.add)
            ins.then_inc(dw_diag_ready, 1)
            step(nc.gpsimd.memset(head_mask[:, :], 1.0))
            same_block(head_mask, HEAD).then_inc(mask_ready, 1)

            for b in range(B):
                roots(rstd[:, 1, b:b + 1], ve[:, 1, b:b + 1], 1, "gn", 1, b)
            for b in range(B):
                pool.wait_ge(x1_ready, 2 * b + 2)
                pool.wait_ge(t_ready[1], b + 1)
                step(nc.gpsimd.tensor_tensor(x1_res[:, b, :], xs[1][:, b, :], res[:, b, :], ALU.add))
            for i in range(2):
                roots(bn_rs[:, i:i + 1], bn_ve[:, i:i + 1], 1, "bn", i)

            def x1_h1_out(b):
                pool.wait_ge(bn2_out_ready, b + 1)
                nc.gpsimd.tensor_tensor(x1_h1[:, b, :], bn2_out[:, b, :], x1_res[:, b, :],
                                        ALU.add).then_inc(x1_h1_ready, 1)

            def gn_root(layer, b):
                roots(rstd[:, layer, b:b + 1], ve[:, layer, b:b + 1], 1, "gn", layer, b)

            for b in range(3):
                x1_h1_out(b)
            gn_root(2, 0)
            x1_h1_out(3)
            for b in range(1, B):
                gn_root(2, b)
            for b in range(B):
                gn_root(3, b)

        @block.scalar
        def _(act):
            act.dma_start(ep[:, :], early).then_inc(early_in, 16)
            act.wait_ge(early_in, 16)
            nc.scalar.activation(bq_s[:, :], ep[:, EC["bq"]], ACT.Copy, scale=SCALE).then_inc(setup_done, 1)
            act.wait_ge(late_in, 16)
            nc.scalar.activation(conv_sign[:, :, :],
                                 lp[:, LC["conv_in"]].rearrange("p (t o) -> p t o", t=TAPS),
                                 ACT.Sign).then_inc(conv_sign_ready, 1)
            act.wait_ge(setup_mm, 1)
            nc.scalar.activation(setup[:, :, :].rearrange("p a c -> p (a c)"), setup_ps[:, 0:2 * C],
                                 ACT.Copy).then_inc(setup_done, 1)

            def q_out(b):
                act.wait_ge(q_mm, b + 1)
                nc.scalar.activation(q[:, b, :], q_ps, ACT.Identity,
                                     bias=bq_s[:, :], scale=SCALE).then_inc(q_ready, 1)

            def softmax(b):
                act.wait_ge(nmax_ready, b + 1)
                for par in range(2):
                    nc.scalar.activation(prob[:, b, par, :], s_ps[b % 2][:, par * N:(par + 1) * N],
                                         ACT.Exp, bias=nmax[:, b, par:par + 1],
                                         accum_out=psum_rows[:, b, par:par + 1]).then_inc(exp_ready, 1)

            def prob_out(b):
                act.wait_ge(pt_mm, b + 1)
                nc.scalar.activation(probT[:, b, :, :, :].rearrange("p j a c -> p (j a c)"),
                                     pt_ps[:, :], ACT.Copy).then_inc(pt_ready, 1)

            act.wait_ge(setup_done, 1)
            q_out(0)
            q_out(1)
            softmax(0)
            q_out(2)
            softmax(1)
            prob_out(0)
            q_out(3)
            softmax(2)
            prob_out(1)
            softmax(3)
            prob_out(2)
            prob_out(3)

            act.wait_ge(borders, 2)
            act.wait_ge(bn1_ready, 1)
            for b in range(B):
                nc.scalar.activation(signs[:, b, 1:H + 1, 1:W + 1],
                                     res[:, b, :].rearrange("p (h w) -> p h w", h=H), ACT.Sign,
                                     bias=bn_shift[:, 0:1], scale=bn_scale[:, 0:1]).then_inc(sign_ready, 1)

            def bn2_apply(b):
                nc.scalar.activation(bn2_out[:, b, :], conv_ps[b], ACT.Identity,
                                     bias=bn_shift[:, 1:2],
                                     scale=bn_scale[:, 1:2]).then_inc(bn2_out_ready, 1)

            def negative_part(b):
                act.wait_ge(h1_ready, b + 1)
                nc.scalar.activation(h1_neg[:, b, :], h1[:, b, :], ACT.Relu,
                                     scale=-1.0).then_inc(h1_neg_ready, 1)

            act.wait_ge(bn2_shift_ready, 1)
            bn2_apply(0)
            bn2_apply(1)
            for b in range(B):
                negative_part(b)
                if b + 2 < B:
                    bn2_apply(b + 2)

            act.wait_ge(l2_consts, 1)

            def relu1(b):
                act.wait_ge(dw_mm, b + 1)
                nc.scalar.activation(h2[:, b, :], dw_ps[b], ACT.Relu, bias=l2_shift[:, 0:1],
                                     scale=l2_scale[:, 0:1]).then_inc(h2_ready, 1)

            def relu2(b):
                act.wait_ge(pw_mm, b + 1)
                nc.scalar.activation(y2[:, b, :], pw_ps[b], ACT.Relu, bias=l2_shift[:, 1:2],
                                     scale=l2_scale[:, 1:2]).then_inc(y2_ready, 1)

            def softmax3(b):
                act.wait_ge(nmax3_ready, b + 1)
                nc.scalar.activation(e3[:, b, :], k_ps, ACT.Exp,
                                     bias=nmax3[:, b:b + 1],
                                     accum_out=sum3[:, b:b + 1]).then_inc(e3_ready, 1)

            def q3_out(b):
                act.wait_ge(q3_mm, b + 1)
                nc.scalar.activation(q3[:, b, :], q_ps, ACT.Copy).then_inc(q3_ready, 1)

            def kt3_out(b):
                act.wait_ge(kt3_mm, b + 1)
                nc.scalar.activation(kt3[:, b, :, :].rearrange("p a c -> p (a c)"), kt_ps,
                                     ACT.Copy).then_inc(kt3_ready, 1)

            def l3(b):
                q3_out(b)
                softmax3(b)
                kt3_out(b)

            relu1(0)
            relu1(1)
            relu2(0)
            relu1(2)
            relu2(1)
            relu1(3)
            relu2(2)
            l3(0)
            relu2(3)
            l3(1)
            l3(2)
            l3(3)

        @block.vector
        def _(dve):
            steps = [0]

            def step(ins):
                steps[0] += 1
                ins.then_inc(dve_step, 1)

            def settle():
                dve.wait_ge(dve_step, steps[0])

            def stats(layer, b):
                src = xs[layer][:, b, :]
                step(nc.vector.bn_stats(st[:, layer, b, :], src))
                settle()
                step(nc.vector.bn_aggr(mv[:, layer, b, :], st[:, layer, b, :]))
                settle()
                nc.vector.scalar_tensor_tensor(
                    out=mv[:, layer, b, 1:2], in0=mv[:, layer, b, 0:1], scalar=mv[:, layer, b, 0:1],
                    in1=mv[:, layer, b, 1:2], op0=ALU.mult, op1=ALU.add).then_inc(stats_ready, 1)

            def group_var(layer, b):
                dve.wait_ge(group_ready, layer * B + b + 1)
                g = gs[:, layer, b, :]
                nc.vector.tensor_copy(g, gn_ps).then_inc(group_out, 1)
                dve.wait_ge(group_out, layer * B + b + 1)
                nc.vector.scalar_tensor_tensor(
                    out=ve[:, layer, b:b + 1], in0=g[:, 0:1], scalar=g[:, 0:1], in1=g[:, 1:2],
                    op0=ALU.mult, op1=ALU.subtract, reverse1=True).then_inc(var_ready, 1)

            def normalise(layer, b, dst):
                dve.wait_ge(rstd_ready, root("gn", layer, b))
                src = xs[layer][:, b, :]
                if layer == 2:
                    src = src.rearrange("p (h w) -> p h w", h=H)
                nc.vector.tensor_scalar(dst, src, gs[:, layer, b, 0:1], rstd[:, layer, b:b + 1],
                                        ALU.subtract, ALU.mult).then_inc(t_ready[layer], 1)

            nc.vector.memset(signs[:, :, :, :].rearrange("p b h w -> p (b h w)").bitcast(fp32),
                             0.0).then_inc(borders, 1)
            nc.vector.memset(pad2[:, :, :, :].rearrange("p b h w -> p (b h w)"), 0.0).then_inc(borders, 1)

            for b in range(B):
                dve.wait_ge(x_in[b], 16)
                stats(0, b)
                if b >= 1:
                    group_var(0, b - 1)
                if b >= 2:
                    normalise(0, b - 2, t0[:, b - 2, :])
            group_var(0, B - 1)
            normalise(0, B - 2, t0[:, B - 2, :])
            normalise(0, B - 1, t0[:, B - 1, :])

            def k_out(b):
                dve.wait_ge(k_mm, b + 1)
                nc.vector.tensor_scalar(k[:, b, :], k_ps, ep[:, EC["bk"]], None,
                                        ALU.add).then_inc(k_ready, 1)

            def v_out(b):
                dve.wait_ge(v_mm, b + 1)
                nc.vector.tensor_tensor(vt[:, b, :, :], v_ps.rearrange("p (a c) -> p a c", a=2),
                                        v_bias.unsqueeze(1).to_broadcast([C, 2, C]),
                                        ALU.add).then_inc(v_ready, 1)

            def row_max(b):
                dve.wait_ge(s_mm, b + 1)
                nc.vector.tensor_reduce(nmax[:, b, :],
                                        s_ps[b % 2][:, :].rearrange("p (a c) -> p a c", a=2),
                                        X_AXIS, ALU.max, negate=True).then_inc(nmax_ready, 1)

            def attend_out(b):
                dve.wait_ge(exp_ready, 2 * b + 2)
                step(nc.vector.reciprocal(rinv[:, b, :], psum_rows[:, b, :]))
                settle()
                dve.wait_ge(o_mm, b + 1)
                for par in range(2):
                    side = slice(par * HALF, (par + 1) * HALF)
                    nc.vector.scalar_tensor_tensor(
                        out=xs[1][:, b, side], in0=o_ps[:, side], scalar=rinv[:, b, par:par + 1],
                        in1=xs[0][:, b, side], op0=ALU.mult, op1=ALU.add).then_inc(x1_ready, 1)
                dve.wait_ge(x1_ready, 2 * b + 2)
                stats(1, b)

            def l1_norm(b):
                group_var(1, b)
                normalise(1, b, res[:, b, :])
                halves = st[:, 1, b, :].rearrange("p (a f) -> p f a", a=2)
                nc.vector.tensor_scalar(halves[:, 1, :], halves[:, 1, :], gs[:, 1, b, 0:1],
                                        rstd[:, 1, b:b + 1], ALU.subtract, ALU.mult)
                step(nc.vector.tensor_scalar(halves[:, 2, :], halves[:, 2, :], rstd[:, 1, b:b + 1],
                                             rstd[:, 1, b:b + 1], ALU.mult, ALU.mult))

            def conv_scale():
                dve.wait_ge(late_in, 16)
                w = lp[:, LC["conv_out"]]
                step(nc.vector.bn_stats(sw_st[:, :], w))
                settle()
                step(nc.vector.bn_aggr(sw_mv[:, :], sw_st[:, :]))
                settle()
                nc.vector.tensor_scalar(sw_var[:, :], sw_mv[:, 1:2], CONV_FAN / (CONV_FAN - 1.0),
                                        None, ALU.mult).then_inc(var_ready, 1)
                step(nc.vector.tensor_scalar(sw_dev[:, :], w, sw_mv[:, 0:1], None, ALU.subtract))
                settle()
                step(nc.vector.tensor_reduce(sw_abs[:, :], sw_dev[:, :], X_AXIS, ALU.add,
                                             apply_absolute_value=True))

            def conv_scale2():
                dve.wait_ge(rstd_ready, root("sw"))
                settle()
                step(nc.vector.tensor_scalar(sw[:, :], sw_abs[:, :], 1.0 / CONV_FAN, sw_rstd[:, :],
                                             ALU.mult, ALU.mult))
                settle()
                step(nc.vector.tensor_tensor(sw_sq[:, :], sw[:, :], sw[:, :], ALU.mult))
                step(nc.vector.tensor_scalar(one_minus_a[:, :], lp[:, LC["prelu"]], -1.0, 1.0,
                                             ALU.mult, ALU.add))
                step(nc.vector.tensor_tensor(sw_gamma[:, :], sw[:, :], lp[:, LC["bn2_gamma"]], ALU.mult))

            dve.wait_ge(early_in, 16)
            dve.wait_ge(setup_done, 2)
            k_out(0)
            v_out(0)
            k_out(1)
            conv_scale()
            row_max(0)
            v_out(1)
            k_out(2)
            row_max(1)
            v_out(2)
            k_out(3)
            row_max(2)
            v_out(3)
            attend_out(0)
            row_max(3)
            conv_scale2()
            attend_out(1)
            l1_norm(0)
            l1_norm(1)
            attend_out(2)
            l1_norm(2)
            attend_out(3)
            l1_norm(3)

            def batchnorm(i, gamma, beta):
                dve.wait_ge(rstd_ready, root("bn", i))
                step(nc.vector.tensor_tensor(bn_scale[:, i:i + 1], bn_rs[:, i:i + 1], gamma, ALU.mult))
                settle()
                step(nc.vector.tensor_tensor(bn_t[:, i:i + 1], bn_mv[:, i, 0:1], bn_scale[:, i:i + 1],
                                             ALU.mult))
                settle()
                return nc.vector.tensor_tensor(bn_shift[:, i:i + 1], beta, bn_t[:, i:i + 1],
                                               ALU.subtract)

            settle()
            step(nc.vector.bn_aggr(bn_mv[:, 0, :], st[:, 1, :, :].rearrange("p b f -> p (b f)")))
            settle()
            nc.vector.tensor_scalar(bn_ve[:, 0:1], bn_mv[:, 0, 1:2], EPS, None,
                                    ALU.add).then_inc(var_ready, 1)
            batchnorm(0, lp[:, LC["bn1_gamma"]], lp[:, LC["bn1_beta"]]).then_inc(bn1_ready, 1)

            for b in range(B):
                dve.wait_ge(conv_mm, b + 1)
                step(nc.vector.bn_stats(bn2_st[:, b, :], conv_ps[b]))
            settle()
            step(nc.vector.bn_aggr(bn_mv[:, 1, :], bn2_st[:, :, :].rearrange("p b f -> p (b f)")))
            settle()
            nc.vector.tensor_scalar(bn_ve[:, 1:2], bn_mv[:, 1, 1:2], sw_sq[:, :], EPS,
                                    ALU.mult, ALU.add).then_inc(var_ready, 1)
            batchnorm(1, sw_gamma[:, :], lp[:, LC["bn2_beta"]]).then_inc(bn2_shift_ready, 1)

            def h1_out(b):
                dve.wait_ge(bn2_out_ready, b + 1)
                nc.vector.tensor_tensor(h1[:, b, :], bn2_out[:, b, :], res[:, b, :],
                                        ALU.add).then_inc(h1_ready, 1)

            def x2_out(b):
                dve.wait_ge(h1_neg_ready, b + 1)
                dve.wait_ge(x1_h1_ready, b + 1)
                step(nc.vector.scalar_tensor_tensor(
                    out=xs[2][:, b, :], in0=h1_neg[:, b, :], scalar=one_minus_a[:, :],
                    in1=x1_h1[:, b, :], op0=ALU.mult, op1=ALU.add))
                settle()
                stats(2, b)

            def l2_norm(b):
                group_var(2, b)
                normalise(2, b, pad2[:, b, 1:H + 1, 1:W + 1])

            def prune1(b):
                dve.wait_ge(h2_ready, b + 1)
                step(nc.vector.tensor_reduce(amax[:, b, 0:1], h2[:, b, :], X_AXIS, ALU.max))
                settle()
                step(nc.vector.tensor_scalar(keep[:, b, 0:1], amax[:, b, 0:1], DW_THRESH, None,
                                             ALU.is_ge))
                settle()
                nc.vector.tensor_scalar(pwT_kept[:, b, :], lp[:, LC["pwT"]], keep[:, b, 0:1], None,
                                        ALU.mult).then_inc(pwT_ready, 1)

            def x3_out(b):
                dve.wait_ge(y2_ready, b + 1)
                step(nc.vector.tensor_reduce(amax[:, b, 1:2], y2[:, b, :], X_AXIS, ALU.max))
                settle()
                step(nc.vector.tensor_scalar(keep[:, b, 1:2], amax[:, b, 1:2], PW_THRESH, None,
                                             ALU.is_ge))
                settle()
                step(nc.vector.scalar_tensor_tensor(out=xs[3][:, b, :], in0=y2[:, b, :],
                                                    scalar=keep[:, b, 1:2], in1=xs[2][:, b, :],
                                                    op0=ALU.mult, op1=ALU.add))
                settle()
                stats(3, b)

            def l3_norm(b):
                group_var(3, b)
                normalise(3, b, t3[:, b, :])

            def k3_max(b):
                dve.wait_ge(k3_mm, b + 1)
                nc.vector.tensor_reduce(nmax3[:, b:b + 1], k_ps, X_AXIS, ALU.max,
                                        negate=True).then_inc(nmax3_ready, 1)

            def v3_out(b):
                dve.wait_ge(vt3_mm, b + 1)
                nc.vector.tensor_copy(vt3[:, b, :, :].rearrange("p a c -> p (a c)"),
                                      vt_ps).then_inc(vt3_ready, 1)

            def context_out(b):
                dve.wait_ge(cx_mm, b + 1)
                nc.vector.tensor_tensor(ctxT[:, b, :], cx_ps, head_mask[:, :],
                                        ALU.mult).then_inc(cx_ready, 1)
                dve.wait_ge(e3_ready, b + 1)
                step(nc.vector.reciprocal(rinv3[:, b:b + 1], sum3[:, b:b + 1]))
                settle()
                dve.wait_ge(pj_mm, b + 1)
                nc.vector.tensor_scalar(proj[:, b, :], pj_ps, rinv3[:, b:b + 1], None,
                                        ALU.mult).then_inc(pj_ready, 1)

            def x4_out(b):
                dve.wait_ge(y3_mm, b + 1)
                nc.vector.scalar_tensor_tensor(out=xs[4][:, b, :], in0=pw_ps[b],
                                               scalar=lp[:, LC["b_out"]], in1=xs[3][:, b, :],
                                               op0=ALU.add, op1=ALU.add).then_inc(x4_ready, 1)

            dve.wait_ge(mask_ready, 1)
            h1_out(0)
            h1_out(1)
            x2_out(0)
            h1_out(2)
            x2_out(1)
            l2_norm(0)
            h1_out(3)
            x2_out(2)
            l2_norm(1)
            x2_out(3)
            prune1(0)
            l2_norm(2)
            l2_norm(3)
            prune1(1)
            x3_out(0)
            prune1(2)
            l3_norm(0)
            x3_out(1)
            prune1(3)
            k3_max(0)
            l3_norm(1)
            x3_out(2)
            v3_out(0)
            k3_max(1)
            l3_norm(2)
            x3_out(3)
            context_out(0)
            v3_out(1)
            l3_norm(3)
            k3_max(2)
            context_out(1)
            v3_out(2)
            x4_out(0)
            k3_max(3)
            context_out(2)
            v3_out(3)
            x4_out(1)
            context_out(3)
            x4_out(2)
            x4_out(3)

        @block.tensor
        def _(pe):
            def fold_weights():
                pe.wait_ge(early_in, 16)
                nc.tensor.matmul(setup_ps[:, 0:C], ep[:, EC["wv"]], ep[:, EC["woT"]],
                                 start=True, stop=True)
                pe.wait_ge(pool_consts, 2)
                nc.tensor.matmul(setup_ps[:, C:2 * C], bias_rows[:, 0, :], ep[:, EC["woT"]],
                                 start=True, stop=False)
                nc.tensor.matmul(setup_ps[:, C:2 * C], bias_rows[:, 1, :], ident[:, :],
                                 start=False, stop=True).then_inc(setup_mm, 1)

            def group_means(layer, b):
                if layer + b:
                    pe.wait_ge(group_out, layer * B + b)
                nc.tensor.matmul(gn_ps, ones[:, :], eps_rhs[:, :], start=True, stop=False)
                pe.wait_ge(stats_ready, layer * B + b + 1)
                nc.tensor.matmul(gn_ps, group_avg[:, :], mv[:, layer, b, :], start=False,
                                 stop=True).then_inc(group_ready, 1)

            def qkv(b):
                pe.wait_ge(t_ready[0], b + 1)
                if b >= 1:
                    pe.wait_ge(q_ready, b)
                nc.tensor.matmul(q_ps, ep[:, EC["wqT"]], t0[:, b, :],
                                 start=True, stop=True).then_inc(q_mm, 1)
                if b >= 1:
                    pe.wait_ge(k_ready, b)
                nc.tensor.matmul(k_ps, ep[:, EC["wkT"]], t0[:, b, :],
                                 start=True, stop=True).then_inc(k_mm, 1)
                if b == 0:
                    pe.wait_ge(setup_done, 2)
                else:
                    pe.wait_ge(v_ready, b)
                for j in range(2):
                    ins = nc.tensor.matmul(v_ps[:, j * C:(j + 1) * C],
                                           t0[:, b, j * C:(j + 1) * C], woT_v,
                                           start=True, stop=True)
                ins.then_inc(v_mm, 1)

            def scores(b):
                pe.wait_ge(q_ready, b + 1)
                pe.wait_ge(k_ready, b + 1)
                if b >= 2:
                    pe.wait_ge(exp_ready, 2 * (b - 1))
                for par in range(2):
                    ins = nc.tensor.matmul(s_ps[b % 2][:, par * N:(par + 1) * N], q[:, b, par:N:2],
                                           k[:, b, :], start=True, stop=True)
                ins.then_inc(s_mm, 1)

            def transpose_prob(b):
                if b >= 1:
                    pe.wait_ge(pt_ready, b)
                for par in range(2):
                    pe.wait_ge(exp_ready, 2 * b + par + 1)
                    for j in range(2):
                        at = (2 * j + par) * C
                        ins = nc.tensor.transpose(pt_ps[:, at:at + C],
                                                  prob[:, b, par, j * C:(j + 1) * C], ident[:, :])
                ins.then_inc(pt_mm, 1)

            def attend(b):
                pe.wait_ge(v_ready, b + 1)
                pe.wait_ge(pt_ready, b + 1)
                if b == 0:
                    pe.wait_ge(setup_done, 2)
                else:
                    pe.wait_ge(x1_ready, 2 * b)
                for par in range(2):
                    for j in range(2):
                        ins = nc.tensor.matmul(o_ps[:, par * C:(par + 1) * C],
                                               probT[:, b, j, par, :], vt[:, b, j, :],
                                               start=(j == 0), stop=(j == 1))
                ins.then_inc(o_mm, 1)

            pe.wait_ge(gn_consts, 1)
            group_means(0, 0)
            fold_weights()
            for b in range(1, B):
                group_means(0, b)
            qkv(0)
            qkv(1)
            scores(0)
            qkv(2)
            scores(1)
            transpose_prob(0)
            qkv(3)
            scores(2)
            attend(0)
            transpose_prob(1)
            scores(3)
            group_means(1, 0)
            attend(1)
            transpose_prob(2)
            group_means(1, 1)
            attend(2)
            transpose_prob(3)
            group_means(1, 2)
            attend(3)
            group_means(1, 3)

            pe.wait_ge(conv_w_ready, 1)
            for b in range(B):
                pe.wait_ge(sign_ready, b + 1)
                for tap in range(TAPS):
                    dy, dx = tap // 3, tap % 3
                    ins = nc.tensor.matmul(conv_ps[b], conv_w[:, tap, :],
                                           signs[:, b, dy:dy + H, dx:dx + W],
                                           start=(tap == 0), stop=(tap == TAPS - 1))
                ins.then_inc(conv_mm, 1)

            def depthwise(b):
                pe.wait_ge(t_ready[2], b + 1)
                if b >= 2:
                    pe.wait_ge(h2_ready, b - 1)
                for tap in range(TAPS):
                    dy, dx = tap // 3, tap % 3
                    ins = nc.tensor.matmul(dw_ps[b], dw_diag[:, tap, :],
                                           pad2[:, b, dy:dy + H, dx:dx + W],
                                           start=(tap == 0), stop=(tap == TAPS - 1))
                ins.then_inc(dw_mm, 1)

            def pointwise(b):
                pe.wait_ge(pwT_ready, b + 1)
                if b >= 2:
                    pe.wait_ge(y2_ready, b - 1)
                nc.tensor.matmul(pw_ps[b], pwT_kept[:, b, :], h2[:, b, :],
                                 start=True, stop=True).then_inc(pw_mm, 1)

            wqkv = [lp[:, LC["wqkvT"].start + i * C:LC["wqkvT"].start + (i + 1) * C] for i in range(3)]

            def qkv3(b):
                pe.wait_ge(t_ready[3], b + 1)
                if b >= 1:
                    pe.wait_ge(e3_ready, b)
                nc.tensor.matmul(k_ps, wqkv[1], t3[:, b, :], start=True, stop=True).then_inc(k3_mm, 1)
                if b >= 1:
                    pe.wait_ge(q3_ready, b)
                nc.tensor.matmul(q_ps, wqkv[0], t3[:, b, :], start=True, stop=True).then_inc(q3_mm, 1)
                if b >= 1:
                    pe.wait_ge(vt3_ready, b)
                for j in range(2):
                    ins = nc.tensor.matmul(vt_ps[:, j * C:(j + 1) * C], t3[:, b, j * C:(j + 1) * C],
                                           wqkv[2], start=True, stop=True)
                ins.then_inc(vt3_mm, 1)

            def transpose_k(b):
                if b == 0:
                    pe.wait_ge(h2_ready, 3)
                else:
                    pe.wait_ge(kt3_ready, b)
                pe.wait_ge(e3_ready, b + 1)
                for j in range(2):
                    ins = nc.tensor.transpose(kt_ps[:, j * C:(j + 1) * C],
                                              e3[:, b, j * C:(j + 1) * C], ident[:, :])
                ins.then_inc(kt3_mm, 1)

            def context(b):
                if b == 0:
                    pe.wait_ge(h2_ready, 4)
                else:
                    pe.wait_ge(pj_ready, b)
                pe.wait_ge(kt3_ready, b + 1)
                pe.wait_ge(vt3_ready, b + 1)
                for j in range(2):
                    ins = nc.tensor.matmul(cx_ps, vt3[:, b, j, :], kt3[:, b, j, :],
                                           start=(j == 0), stop=(j == 1))
                ins.then_inc(cx_mm, 1)

            def project(b):
                pe.wait_ge(cx_ready, b + 1)
                nc.tensor.matmul(pj_ps, ctxT[:, b, :], lp[:, LC["woutT"]],
                                 start=True, stop=True).then_inc(pj_mm, 1)

            def output(b):
                pe.wait_ge(pj_ready, b + 1)
                if b < 2:
                    pe.wait_ge(y2_ready, b + 3)
                else:
                    pe.wait_ge(x4_ready, b - 1)
                nc.tensor.matmul(pw_ps[b], proj[:, b, :], q3[:, b, :],
                                 start=True, stop=True).then_inc(y3_mm, 1)

            group_means(2, 0)
            group_means(2, 1)
            pe.wait_ge(dw_diag_ready, 1)
            depthwise(0)
            group_means(2, 2)
            depthwise(1)
            group_means(2, 3)
            pointwise(0)
            depthwise(2)
            pointwise(1)
            group_means(3, 0)
            depthwise(3)
            pointwise(2)
            group_means(3, 1)
            qkv3(0)
            pointwise(3)
            qkv3(1)
            group_means(3, 2)
            transpose_k(0)
            context(0)
            group_means(3, 3)
            project(0)
            qkv3(2)
            transpose_k(1)
            output(0)
            context(1)
            project(1)
            qkv3(3)
            transpose_k(2)
            output(1)
            context(2)
            project(2)
            transpose_k(3)
            output(2)
            context(3)
            project(3)
            output(3)


def kernel(**inputs):
    import numpy as np
    import concourse.bacc as bacc
    from concourse.bass_utils import run_bass_kernel_spmd

    def arr(name):
        return np.ascontiguousarray(np.asarray(inputs[name]))

    def col(*names):
        return np.stack([arr(n) for n in names], axis=1)

    conv = arr("L1_conv_conv_w").reshape(C // CONV_GROUP, CONV_GROUP, CONV_GROUP, TAPS)
    early = [arr("L0_conv_Wq").T, arr("L0_conv_Wk").T, arr("L0_conv_Wv"), arr("L0_conv_Wo").T,
             col("L0_conv_bq", "L0_conv_bk", "L0_conv_bv", "L0_conv_bo")]
    late = [conv.transpose(0, 2, 3, 1).reshape(C, TAPS * CONV_GROUP),
            arr("L1_conv_conv_w").reshape(C, CONV_FAN), arr("L2_conv_dw_w").reshape(C, TAPS),
            col("L1_conv_bn1_gamma", "L1_conv_bn1_beta", "L1_conv_bn2_gamma", "L1_conv_bn2_beta",
                "L1_conv_prelu_a", "L2_conv_dw_b", "L2_conv_pw_b", "L2_conv_bn1_g", "L2_conv_bn2_g",
                "L2_conv_bn1_b", "L2_conv_bn2_b", "L2_conv_bn1_m", "L2_conv_bn2_m", "L2_conv_bn1_v",
                "L2_conv_bn2_v", "L3_conv_b_out"),
            arr("L2_conv_pw_w").reshape(C, C).T, arr("L3_conv_w_qkv").T, arr("L3_conv_w_out").T]
    arrays = {"x": arr("x"), "early": np.ascontiguousarray(np.concatenate(early, axis=1)),
              "late": np.ascontiguousarray(np.concatenate(late, axis=1))}

    nc = bacc.Bacc("TRN2", target_bir_lowering=False, num_devices=1)
    args = [nc.dram_tensor(f"in_{name}", a.shape, mybir.dt.float32, kind="ExternalInput").ap()
            for name, a in arrays.items()]
    out = nc.dram_tensor("out", (B, C, H, W), mybir.dt.float32, kind="ExternalOutput").ap()
    build(nc, *args, out)
    r = run_bass_kernel_spmd(nc, [{f"in_{name}": a for name, a in arrays.items()}], core_ids=[0])
    return r.results[0]["out"]
```

```python
import concourse.bass as bass
from concourse import mybir
from contextlib import ExitStack

B, C, H, W = 4, 128, 16, 16
N = H * W
HALF = N // 2
TAPS = 9
PH, PW = H + 2, W + 2
GN_GROUP = C // 32
CONV_GROUP = C // 16
HEAD = 16
CONV_FAN = CONV_GROUP * TAPS
EPS = 1e-5
PE_TAPS = 5
DW_THRESH = 4.0
PW_THRESH = 0.001

EARLY = [("wqT", C), ("wkT", C), ("wv", C), ("woT", C), ("bq", 1), ("bk", 1), ("bv", 1), ("bo", 1)]
LATE = [("conv_in", TAPS * CONV_GROUP), ("conv_out", CONV_FAN), ("dw", TAPS),
        ("bn1_gamma", 1), ("bn1_beta", 1), ("bn2_gamma", 1), ("bn2_beta", 1), ("prelu", 1),
        ("l2_bias", 2), ("l2_g", 2), ("l2_b", 2), ("l2_m", 2), ("l2_v", 2), ("b_out", 1),
        ("pwT", C), ("wqkvT", 3 * C), ("woutT", C)]


def columns(fields):
    at, out = 0, {}
    for name, width in fields:
        out[name] = slice(at, at + width)
        at += width
    return out, at


def build(nc, x, early, late, out):
    fp32, bf16 = mybir.dt.float32, mybir.dt.bfloat16
    ALU = mybir.AluOpType
    ACT = mybir.ActivationFunctionType
    X_AXIS = mybir.AxisListType.X
    EC, EARLY_W = columns(EARLY)
    LC, LATE_W = columns(LATE)
    x_v = x.rearrange("b c h w -> b c (h w)")
    out_v = out.rearrange("b c h w -> b c (h w)")

    ctx = ExitStack()
    with ctx:
        def sb(name, shape, dt=fp32):
            return ctx.enter_context(nc.sbuf_tensor(name, shape, dt))

        def sem(name):
            return ctx.enter_context(nc.semaphore(name))

        ep = sb("early_params", [C, EARLY_W])
        lp = sb("late_params", [C, LATE_W])
        ident = sb("ident", [C, C])
        warm = sb("warm", [C, N], bf16)
        ones = sb("ones", [C, C])
        group_avg = sb("group_avg", [C, C])
        group_sum = sb("group_sum", [C, C])
        head_mask = sb("head_mask", [C, C])
        conv_mask = sb("conv_mask", [C, C // CONV_GROUP], bf16)
        eps_row = sb("eps_row", [C, 2])
        minus_half = sb("minus_half", [C, B])
        bias_rows = sb("bias_rows", [C, 2, C])
        setup = sb("setup", [C, 2, C])
        woT_v = setup[:, 0, :]
        v_bias = setup[:, 1, :]
        bq_s = sb("bq_scaled", [C, 1])
        conv_sign = sb("conv_sign", [C, TAPS, CONV_GROUP], bf16)
        conv_w = sb("conv_blocks", [C, TAPS, C], bf16)
        dw_diag = sb("dw_diag", [C, PE_TAPS, C])
        sw_st = sb("sw_stats", [C, 6])
        sw_mv = sb("sw_mean_var", [C, 2])
        sw_dev = sb("sw_deviation", [C, CONV_FAN])
        sw_abs = sb("sw_abs_sum", [C, 1])
        sw_var = sb("sw_var", [C, 1])
        sw_rstd = sb("sw_rstd", [C, 1])
        sw = sb("sw", [C, 1])
        sw_sq = sb("sw_squared", [C, 1])
        sw_gamma = sb("sw_gamma", [C, 1])
        l2_ve = sb("l2_var_eps", [C, 2])
        l2_rs = sb("l2_rstd", [C, 2])
        l2_scale = sb("l2_scale", [C, 2])
        l2_t = sb("l2_t", [C, 2])
        l2_t2 = sb("l2_t2", [C, 2])
        l2_shift = sb("l2_shift", [C, 2])

        xs = [sb(f"x{i}", [C, B, N]) for i in range(5)]
        xb = sb("x_bias", [C, B, N])
        t0 = sb("t0", [C, B, N])
        res = sb("res", [C, B, N])
        pad2 = sb("pad2", [C, B, PH, PW])
        t3 = sb("t3", [C, B, N])
        signs = sb("signs", [C, B, PH, PW], bf16)
        q = sb("q", [C, B, N])
        k = sb("k", [C, B, N])
        vt = sb("vt", [C, B, 2, C])
        nmax = sb("nmax", [C, B, 2])
        prob = sb("prob", [C, B, 2, N])
        psum_rows = sb("prob_sum", [C, B, 2])
        rinv = sb("rinv", [C, B, 2])
        probT = sb("probT", [C, B, 2, 2, C])
        x1_res = sb("x1_res", [C, B, N])
        bn2_out = sb("bn2_out", [C, B, N])
        h1 = sb("h1", [C, B, N])
        x1_h1 = sb("x1_h1", [C, B, N])
        h1_neg = sb("h1_neg", [C, B, N])
        one_minus_a = sb("one_minus_a", [C, 1])
        dw_acc = sb("dw_acc", [C, B, TAPS - PE_TAPS, N])
        dw_sum = sb("dw_sum", [C, B, N])
        h2 = sb("h2", [C, B, N])
        amax = sb("amax", [C, B, 2])
        keep = sb("keep", [C, B, 2])
        pwT_kept = sb("pwT_kept", [C, B, C])
        y2 = sb("y2", [C, B, N])
        q3 = sb("q3", [C, B, N])
        nmax3 = sb("nmax3", [C, B])
        e3 = sb("e3", [C, B, N])
        sum3 = sb("sum3", [C, B])
        rinv3 = sb("rinv3", [C, B])
        vt3 = sb("vt3", [C, B, 2, C])
        kt3 = sb("kt3", [C, B, 2, C])
        ctxT = sb("ctxT", [C, B, C])
        proj = sb("proj", [C, B, C])

        st = sb("gn_stats", [C, 4, B, 6])
        mv = sb("gn_mean_sq", [C, 4, B, 2])
        msq0 = sb("gn_mean_squared", [C, B])
        squares = sb("squares", [C, 2, B, N])
        gs = sb("gn_group", [C, 4, B, 2])
        ve = sb("gn_var_eps", [C, 4, B])
        rstd = sb("gn_rstd", [C, 4, B])
        bn_mv = sb("bn_mean_var", [C, 2, 2])
        bn_ve = sb("bn_var_eps", [C, 2])
        bn_rs = sb("bn_rstd", [C, 2])
        bn_scale = sb("bn_scale", [C, 2])
        bn_shift = sb("bn_shift", [C, 2])
        bn2_st = sb("bn2_stats", [C, B, 6])

        banks = [ctx.enter_context(nc.psum_tensor(f"bank{i}", [C, 512], fp32)) for i in range(8)]

        q_ps, k_ps = banks[0][:, 0:N], banks[1][:, 0:N]
        v_ps = banks[2][:, 0:N]
        s_ps = [banks[3], banks[4]]
        pt_ps = banks[5]
        o_ps = banks[6][:, 0:N]
        setup_ps = banks[6]
        warm_ps = banks[4]
        conv_ps = [banks[i][:, 0:N] for i in (0, 1, 2, 5)]
        dw_ps = [banks[3 + b % 2][:, 0:N] for b in range(B)]
        pw_ps = banks[6][:, 0:N]
        vt_ps = kt_ps = banks[5][:, 0:N]
        pj_ps = banks[2][:, 0:C]
        y_ps = banks[2][:, 0:N]
        gn_ps = banks[7]
        cx_ps = banks[7][:, 0:C]

        x_in = [sem("x_in0"), sem("x_in1")]
        early_in = sem("early_in")
        late_in = sem("late_in")
        stored = sem("stored")
        pool_step = sem("pool_step")
        dve_step = sem("dve_step")
        warm_ready = sem("warm_ready")
        gn_consts = sem("gn_consts")
        pool_consts = sem("pool_consts")
        masks = sem("masks")
        conv_w_ready = sem("conv_w_ready")
        dw_diag_ready = sem("dw_diag_ready")
        l2_consts = sem("l2_consts")
        borders = sem("borders")
        conv_sign_ready = sem("conv_sign_ready")
        setup_mm = sem("setup_mm")
        setup_done = sem("setup_done")
        sw_var_ready = sem("sw_var_ready")
        sw_rstd_ready = sem("sw_rstd_ready")
        stats_ready = [sem(f"stats_ready{i}") for i in range(4)]
        group_ready = [sem(f"group_ready{i}") for i in range(4)]
        group_read = [sem(f"group_read{i}") for i in range(4)]
        var_ready = [sem(f"var_ready{i}") for i in range(4)]
        rstd_ready = [sem(f"rstd_ready{i}") for i in range(4)]
        t_ready = [sem(f"t_ready{i}") for i in range(4)]
        q_mm, k_mm, v_mm = sem("q_mm"), sem("k_mm"), sem("v_mm")
        q_ready, k_ready, v_ready = sem("q_ready"), sem("k_ready"), sem("v_ready")
        s_mm = sem("s_mm")
        nmax_ready = sem("nmax_ready")
        exp_ready = sem("exp_ready")
        pt_mm, pt_ready = sem("pt_mm"), sem("pt_ready")
        o_mm = sem("o_mm")
        xb_ready = sem("xb_ready")
        x1_ready = sem("x1_ready")
        bn_var_ready, bn_rstd_ready = sem("bn_var_ready"), sem("bn_rstd_ready")
        bn_shift_ready = sem("bn_shift_ready")
        sign_ready = sem("sign_ready")
        conv_mm = sem("conv_mm")
        bn2_st_ready = sem("bn2_st_ready")
        bn2_out_ready = sem("bn2_out_ready")
        h1_ready = sem("h1_ready")
        h1_neg_ready = sem("h1_neg_ready")
        x1_h1_ready = sem("x1_h1_ready")
        x2_ready = sem("x2_ready")
        dw_mm = sem("dw_mm")
        dw_acc_ready = sem("dw_acc_ready")
        dw_ready = sem("dw_ready")
        h2_ready = sem("h2_ready")
        pwT_ready = sem("pwT_ready")
        pw_mm = sem("pw_mm")
        y2_ready = sem("y2_ready")
        x3_ready = sem("x3_ready")
        k3_mm, q3_mm, vt3_mm = sem("k3_mm"), sem("q3_mm"), sem("vt3_mm")
        nmax3_ready = sem("nmax3_ready")
        q3_ready, e3_ready, vt3_ready = sem("q3_ready"), sem("e3_ready"), sem("vt3_ready")
        kt3_mm, kt3_ready = sem("kt3_mm"), sem("kt3_ready")
        cx_mm, cx_ready = sem("cx_mm"), sem("cx_ready")
        pj_mm, pj_ready = sem("pj_mm"), sem("pj_ready")
        y3_mm = sem("y3_mm")
        x4_ready = sem("x4_ready")

        SCALE = float(C) ** -0.5

        block = ctx.enter_context(nc.Block())

        @block.sync
        def _(sp):
            sp.dma_start(xs[0][:, 0, :], x_v[0]).then_inc(x_in[0], 16)
            sp.dma_start(xs[0][:, 1:B, :], x_v[1:B].rearrange("b c n -> c b n")).then_inc(x_in[1], 16)
            sp.dma_start(ep[:, :], early).then_inc(early_in, 16)
            sp.dma_start(lp[:, :], late).then_inc(late_in, 16)
            for b in range(B):
                sp.wait_ge(x4_ready, b + 1)
                sp.dma_start(out_v[b], xs[4][:, b, :]).then_inc(stored, 16)
            sp.wait_ge(stored, 16 * B)

        @block.gpsimd
        def _(pool):
            steps = [0]

            def step(ins):
                steps[0] += 1
                ins.then_inc(pool_step, 1)
                pool.wait_ge(pool_step, steps[0])

            def same_block(tile, size):
                inner = [[0, size]] if tile.shape[1] == C else []
                step(nc.gpsimd.affine_select(out=tile[:, :], in_=tile[:, :], compare_op=ALU.is_ge,
                                             fill=0.0, base=0, pattern=[[-size, C // size]] + inner,
                                             channel_multiplier=1))
                return nc.gpsimd.affine_select(out=tile[:, :], in_=tile[:, :], compare_op=ALU.is_ge,
                                               fill=0.0, base=size - 1,
                                               pattern=[[size, C // size]] + inner,
                                               channel_multiplier=-1)

            nc.gpsimd.memset(warm[:, :], 1.0).then_inc(warm_ready, 1)
            nc.gpsimd.memset(ones[:, :], 1.0)
            nc.gpsimd.memset(eps_row[:, 0:1], 0.0)
            nc.gpsimd.memset(eps_row[:, 1:2], EPS)
            nc.gpsimd.memset(minus_half[:, :], -0.5)
            step(nc.gpsimd.memset(group_avg[:, :], 1.0 / GN_GROUP))
            same_block(group_avg, GN_GROUP).then_inc(gn_consts, 1)
            step(nc.gpsimd.memset(ident[:, :], 0.0))
            nc.gpsimd.affine_select(out=ident[:, :], in_=ident[:, :], compare_op=ALU.not_equal,
                                    fill=1.0, base=0, pattern=[[-1, C]],
                                    channel_multiplier=1).then_inc(pool_consts, 1)

            def root(out_ap, in_ap):
                n = in_ap.shape[1]
                return nc.gpsimd.tensor_tensor(out_ap, in_ap, minus_half[:, 0:n], ALU.pow)

            pool.wait_ge(var_ready[0], 1)
            root(rstd[:, 0, 0:1], ve[:, 0, 0:1]).then_inc(rstd_ready[0], 1)
            pool.wait_ge(early_in, 16)
            for i, name in enumerate(("bv", "bo")):
                ins = nc.gpsimd.tensor_scalar(bias_rows[:, i, :], ones[:, :], ep[:, EC[name]], 0.0,
                                              ALU.mult, ALU.add)
            ins.then_inc(pool_consts, 1)

            pool.wait_ge(var_ready[0], 2)
            root(rstd[:, 0, 1:B], ve[:, 0, 1:B]).then_inc(rstd_ready[0], 1)

            pool.wait_ge(setup_done, 2)
            for b in range(B):
                pool.wait_ge(x_in[min(b, 1)], 16)
                nc.gpsimd.tensor_tensor(xb[:, b, :].rearrange("p (a c) -> p a c", a=2),
                                        xs[0][:, b, :].rearrange("p (a c) -> p a c", a=2),
                                        v_bias.unsqueeze(1).to_broadcast([C, 2, C]),
                                        ALU.add).then_inc(xb_ready, 1)

            step(nc.gpsimd.memset(conv_mask[:, :], 1.0))
            step(same_block(conv_mask, CONV_GROUP))
            pool.wait_ge(conv_sign_ready, 1)
            groups = C // CONV_GROUP
            for tap in range(TAPS):
                ins = nc.gpsimd.tensor_tensor(
                    conv_w[:, tap, :].rearrange("p (g o) -> p g o", o=CONV_GROUP),
                    conv_sign[:, tap, :].unsqueeze(1).to_broadcast([C, groups, CONV_GROUP]),
                    conv_mask[:, :].unsqueeze(2).to_broadcast([C, groups, CONV_GROUP]), ALU.mult)
            ins.then_inc(conv_w_ready, 1)
            pool.wait_ge(sw_var_ready, 1)
            root(sw_rstd[:, :], sw_var[:, :]).then_inc(sw_rstd_ready, 1)
            pool.wait_ge(late_in, 16)
            step(nc.gpsimd.tensor_scalar(l2_ve[:, :], lp[:, LC["l2_v"]], 1.0, EPS, ALU.mult, ALU.add))
            step(root(l2_rs[:, :], l2_ve[:, :]))
            nc.gpsimd.tensor_tensor(l2_t[:, :], lp[:, LC["l2_bias"]], lp[:, LC["l2_m"]], ALU.subtract)
            step(nc.gpsimd.tensor_tensor(l2_scale[:, :], l2_rs[:, :], lp[:, LC["l2_g"]], ALU.mult))
            step(nc.gpsimd.tensor_tensor(l2_t2[:, :], l2_t[:, :], l2_scale[:, :], ALU.mult))
            nc.gpsimd.tensor_tensor(l2_shift[:, :], l2_t2[:, :], lp[:, LC["l2_b"]],
                                    ALU.add).then_inc(l2_consts, 1)
            for tap in range(PE_TAPS):
                ins = nc.gpsimd.tensor_scalar(dw_diag[:, tap, :], ident[:, :],
                                              lp[:, LC["dw"].start + tap:LC["dw"].start + tap + 1],
                                              0.0, ALU.mult, ALU.add)
            ins.then_inc(dw_diag_ready, 1)
            nc.gpsimd.tensor_scalar(group_sum[:, :], group_avg[:, :], 1.0 / N, 0.0, ALU.mult, ALU.add)
            step(nc.gpsimd.memset(head_mask[:, :], 1.0))
            same_block(head_mask, HEAD).then_inc(masks, 1)

            def gn_root(layer, b):
                pool.wait_ge(var_ready[layer], b + 1)
                root(rstd[:, layer, b:b + 1], ve[:, layer, b:b + 1]).then_inc(rstd_ready[layer], 1)

            def bn_root(i):
                pool.wait_ge(bn_var_ready, i + 1)
                root(bn_rs[:, i:i + 1], bn_ve[:, i:i + 1]).then_inc(bn_rstd_ready, 1)

            def x1_res_out(b):
                pool.wait_ge(t_ready[1], b + 1)
                steps[0] += 1
                nc.gpsimd.tensor_tensor(x1_res[:, b, :], xs[1][:, b, :], res[:, b, :],
                                        ALU.add).then_inc(pool_step, 1)

            def x1_h1_out(b):
                pool.wait_ge(bn2_out_ready, b + 1)
                pool.wait_ge(pool_step, steps[0])
                nc.gpsimd.tensor_tensor(x1_h1[:, b, :], bn2_out[:, b, :], x1_res[:, b, :],
                                        ALU.add).then_inc(x1_h1_ready, 1)

            gn_root(1, 0)
            gn_root(1, 1)
            x1_res_out(0)
            gn_root(1, 2)
            gn_root(1, 3)
            x1_res_out(1)
            x1_res_out(2)
            bn_root(0)
            x1_res_out(3)
            bn_root(1)
            x1_h1_out(0)
            x1_h1_out(1)
            x1_h1_out(2)
            x1_h1_out(3)
            gn_root(2, 0)
            gn_root(2, 1)
            gn_root(2, 2)
            gn_root(2, 3)
            gn_root(3, 0)
            gn_root(3, 1)
            gn_root(3, 2)
            gn_root(3, 3)
        @block.scalar
        def _(act):
            act.wait_ge(early_in, 16)
            nc.scalar.activation(bq_s[:, :], ep[:, EC["bq"]], ACT.Copy, scale=SCALE).then_inc(setup_done, 1)
            act.wait_ge(late_in, 16)
            nc.scalar.activation(conv_sign[:, :, :],
                                 lp[:, LC["conv_in"]].rearrange("p (t o) -> p t o", t=TAPS),
                                 ACT.Sign).then_inc(conv_sign_ready, 1)
            act.wait_ge(setup_mm, 1)
            nc.scalar.activation(setup[:, :, :].rearrange("p a c -> p (a c)"), setup_ps[:, 0:2 * C],
                                 ACT.Copy).then_inc(setup_done, 1)

            def q_out(b):
                act.wait_ge(q_mm, b + 1)
                nc.scalar.activation(q[:, b, :], q_ps, ACT.Identity,
                                     bias=bq_s[:, :], scale=SCALE).then_inc(q_ready, 1)

            def softmax(b):
                act.wait_ge(nmax_ready, b + 1)
                for par in range(2):
                    nc.scalar.activation(prob[:, b, par, :], s_ps[b % 2][:, par * N:(par + 1) * N],
                                         ACT.Exp, bias=nmax[:, b, par:par + 1],
                                         accum_out=psum_rows[:, b, par:par + 1]).then_inc(exp_ready, 1)

            def v_out(b):
                act.wait_ge(v_mm, b + 1)
                nc.scalar.activation(vt[:, b, :, :].rearrange("p a c -> p (a c)"), v_ps,
                                     ACT.Copy).then_inc(v_ready, 1)

            def prob_out(b):
                act.wait_ge(pt_mm, b + 1)
                nc.scalar.activation(probT[:, b, :, :, :].rearrange("p j a c -> p (j a c)"),
                                     pt_ps[:, :], ACT.Copy).then_inc(pt_ready, 1)

            def sign_out(b):
                if b == 0:
                    act.wait_ge(borders, 1)
                    act.wait_ge(bn_shift_ready, 1)
                act.wait_ge(t_ready[1], b + 1)
                nc.scalar.activation(signs[:, b, 1:H + 1, 1:W + 1],
                                     res[:, b, :].rearrange("p (h w) -> p h w", h=H), ACT.Sign,
                                     bias=bn_shift[:, 0:1], scale=bn_scale[:, 0:1]).then_inc(sign_ready, 1)

            def bn2_apply(b):
                if b == 0:
                    act.wait_ge(bn_shift_ready, 2)
                nc.scalar.activation(bn2_out[:, b, :], conv_ps[b], ACT.Identity,
                                     bias=bn_shift[:, 1:2],
                                     scale=bn_scale[:, 1:2]).then_inc(bn2_out_ready, 1)

            def negative_part(b):
                act.wait_ge(h1_ready, b + 1)
                nc.scalar.activation(h1_neg[:, b, :], h1[:, b, :], ACT.Relu,
                                     scale=-1.0).then_inc(h1_neg_ready, 1)

            def square_sum(layer, b):
                act.wait_ge(x2_ready if layer == 2 else x3_ready, b + 1)
                nc.scalar.activation(squares[:, layer - 2, b, :], xs[layer][:, b, :], ACT.Square,
                                     accum_out=mv[:, layer, b, 1:2]).then_inc(stats_ready[layer], 1)

            def dw_first_tap(b):
                act.wait_ge(t_ready[2], b + 1)
                if b >= 1:
                    act.wait_ge(dw_acc_ready, (TAPS - PE_TAPS) * b)
                dy, dx = PE_TAPS // 3, PE_TAPS % 3
                nc.scalar.activation(
                    dw_acc[:, b, 0, :].rearrange("p (h w) -> p h w", h=H),
                    pad2[:, b, dy:dy + H, dx:dx + W], ACT.Copy,
                    scale=lp[:, LC["dw"].start + PE_TAPS:LC["dw"].start + PE_TAPS + 1]
                ).then_inc(dw_acc_ready, 1)

            def relu1(b):
                if b == 0:
                    act.wait_ge(l2_consts, 1)
                act.wait_ge(dw_ready, b + 1)
                nc.scalar.activation(h2[:, b, :], dw_sum[:, b, :], ACT.Relu,
                                     bias=l2_shift[:, 0:1], scale=l2_scale[:, 0:1]).then_inc(h2_ready, 1)

            def relu2(b):
                act.wait_ge(pw_mm, b + 1)
                nc.scalar.activation(y2[:, b, :], pw_ps, ACT.Relu, bias=l2_shift[:, 1:2],
                                     scale=l2_scale[:, 1:2]).then_inc(y2_ready, 1)

            def softmax3(b):
                act.wait_ge(nmax3_ready, b + 1)
                nc.scalar.activation(e3[:, b, :], k_ps, ACT.Exp, bias=nmax3[:, b:b + 1],
                                     accum_out=sum3[:, b:b + 1]).then_inc(e3_ready, 1)

            def q3_out(b):
                act.wait_ge(q3_mm, b + 1)
                nc.scalar.activation(q3[:, b, :], q_ps, ACT.Copy).then_inc(q3_ready, 1)

            def v3_out(b):
                act.wait_ge(vt3_mm, b + 1)
                nc.scalar.activation(vt3[:, b, :, :].rearrange("p a c -> p (a c)"), vt_ps,
                                     ACT.Copy).then_inc(vt3_ready, 1)

            def kt3_out(b):
                act.wait_ge(kt3_mm, b + 1)
                nc.scalar.activation(kt3[:, b, :, :].rearrange("p a c -> p (a c)"), kt_ps,
                                     ACT.Copy).then_inc(kt3_ready, 1)

            act.wait_ge(setup_done, 1)
            q_out(0)
            v_out(0)
            softmax(0)
            v_out(1)
            q_out(1)
            prob_out(0)
            q_out(2)
            softmax(1)
            q_out(3)
            softmax(2)
            prob_out(1)
            v_out(2)
            softmax(3)
            prob_out(2)
            v_out(3)
            prob_out(3)
            sign_out(0)
            sign_out(1)
            sign_out(2)
            sign_out(3)
            bn2_apply(0)
            bn2_apply(1)
            bn2_apply(2)
            negative_part(0)
            negative_part(1)
            negative_part(2)
            bn2_apply(3)
            square_sum(2, 0)
            square_sum(2, 1)
            negative_part(3)
            square_sum(2, 2)
            square_sum(2, 3)
            dw_first_tap(0)
            dw_first_tap(1)
            relu1(0)
            dw_first_tap(2)
            relu1(1)
            relu2(0)
            relu2(1)
            relu1(2)
            dw_first_tap(3)
            square_sum(3, 0)
            square_sum(3, 1)
            relu2(2)
            relu1(3)
            square_sum(3, 2)
            v3_out(0)
            softmax3(0)
            q3_out(0)
            relu2(3)
            kt3_out(0)
            q3_out(1)
            softmax3(1)
            v3_out(1)
            q3_out(2)
            square_sum(3, 3)
            kt3_out(1)
            softmax3(2)
            v3_out(2)
            kt3_out(2)
            softmax3(3)
            q3_out(3)
            v3_out(3)
            kt3_out(3)
        @block.vector
        def _(dve):
            steps = [0]
            made = {}

            def step(ins, *name):
                steps[0] += 1
                made[name] = steps[0]
                ins.then_inc(dve_step, 1)

            def settle(*name):
                dve.wait_ge(dve_step, made[name])

            nc.vector.memset(signs[:, :, :, :].rearrange("p b h w -> p (b h w)").bitcast(fp32),
                             0.0).then_inc(borders, 1)
            step(nc.vector.memset(pad2[:, :, :, :].rearrange("p b h w -> p (b h w)"), 0.0), "pad2")


            def gn_stats(layer, b):
                step(nc.vector.bn_stats(st[:, layer, b, :], xs[layer][:, b, :]), "stats", layer, b)

            def gn_aggr(layer, b):
                settle("stats", layer, b)
                step(nc.vector.bn_aggr(mv[:, layer, b, :], st[:, layer, b, :]), "aggr", layer, b)

            def gn_mean_sq(layer, b):
                settle("aggr", layer, b)
                nc.vector.scalar_tensor_tensor(
                    out=mv[:, layer, b, 1:2], in0=mv[:, layer, b, 0:1], scalar=mv[:, layer, b, 0:1],
                    in1=mv[:, layer, b, 1:2], op0=ALU.mult, op1=ALU.add).then_inc(stats_ready[layer], 1)

            def group_out(layer, b):
                dve.wait_ge(group_ready[layer], b + 1)
                nc.vector.tensor_tensor(gs[:, layer, b, :], gn_ps[:, 0:2], eps_row[:, :],
                                        ALU.add).then_inc(group_read[layer], 1)

            def group_var(layer, b):
                dve.wait_ge(group_read[layer], b + 1)
                g = gs[:, layer, b, :]
                nc.vector.scalar_tensor_tensor(
                    out=ve[:, layer, b:b + 1], in0=g[:, 0:1], scalar=g[:, 0:1], in1=g[:, 1:2],
                    op0=ALU.mult, op1=ALU.subtract, reverse1=True).then_inc(var_ready[layer], 1)

            def normalise(layer, b, dst, roots_done):
                dve.wait_ge(rstd_ready[layer], roots_done)
                src = xs[layer][:, b, :]
                if layer == 2:
                    src = src.rearrange("p (h w) -> p h w", h=H)
                nc.vector.tensor_scalar(dst, src, gs[:, layer, b, 0:1], rstd[:, layer, b:b + 1],
                                        ALU.subtract, ALU.mult).then_inc(t_ready[layer], 1)

            dve.wait_ge(x_in[0], 16)
            gn_stats(0, 0)
            gn_aggr(0, 0)
            gn_mean_sq(0, 0)
            dve.wait_ge(x_in[1], 16)
            gn_stats(0, 1)
            dve.wait_ge(pool_consts, 1)
            group_out(0, 0)
            gn_stats(0, 2)
            group_var(0, 0)
            gn_stats(0, 3)
            for b in range(1, B):
                gn_aggr(0, b)
            normalise(0, 0, t0[:, 0, :], 1)
            settle("aggr", 0, B - 1)
            step(nc.vector.tensor_tensor(msq0[:, 1:B], mv[:, 0, 1:B, 0], mv[:, 0, 1:B, 0], ALU.mult),
                 "msq0")
            settle("msq0")
            nc.vector.tensor_tensor(mv[:, 0, 1:B, 1], mv[:, 0, 1:B, 1], msq0[:, 1:B],
                                    ALU.add).then_inc(stats_ready[0], 1)
            dve.wait_ge(group_ready[0], 2)
            nc.vector.tensor_tensor(
                gs[:, 0, 1:B, :], gn_ps[:, 0:2 * (B - 1)].rearrange("p (b f) -> p b f", f=2),
                eps_row[:, :].unsqueeze(1).to_broadcast([C, B - 1, 2]),
                ALU.add).then_inc(group_read[0], 1)
            dve.wait_ge(group_read[0], 2)
            step(nc.vector.tensor_tensor(msq0[:, 1:B], gs[:, 0, 1:B, 0], gs[:, 0, 1:B, 0], ALU.mult),
                 "gm_sq")
            settle("gm_sq")
            nc.vector.tensor_tensor(ve[:, 0, 1:B], gs[:, 0, 1:B, 1], msq0[:, 1:B],
                                    ALU.subtract).then_inc(var_ready[0], 1)
            w_out = lp[:, LC["conv_out"]]

            def sw_stats():
                dve.wait_ge(late_in, 16)
                step(nc.vector.bn_stats(sw_st[:, :], w_out), "sw_st")
                step(nc.vector.tensor_scalar(one_minus_a[:, :], lp[:, LC["prelu"]], -1.0, 1.0,
                                             ALU.mult, ALU.add), "one_minus_a")

            def sw_aggr():
                settle("sw_st")
                step(nc.vector.bn_aggr(sw_mv[:, :], sw_st[:, :]), "sw_mv")

            def sw_variance():
                settle("sw_mv")
                nc.vector.tensor_scalar(sw_var[:, :], sw_mv[:, 1:2], CONV_FAN / (CONV_FAN - 1.0),
                                        None, ALU.mult).then_inc(sw_var_ready, 1)
                step(nc.vector.tensor_scalar(sw_dev[:, :], w_out, sw_mv[:, 0:1], None, ALU.subtract),
                     "sw_dev")

            def sw_abs_sum():
                settle("sw_dev")
                step(nc.vector.tensor_reduce(sw_abs[:, :], sw_dev[:, :], X_AXIS, ALU.add,
                                             apply_absolute_value=True), "sw_abs")

            def sw_scale():
                dve.wait_ge(sw_rstd_ready, 1)
                settle("sw_abs")
                step(nc.vector.tensor_scalar(sw[:, :], sw_abs[:, :], 1.0 / CONV_FAN, sw_rstd[:, :],
                                             ALU.mult, ALU.mult), "sw")

            def sw_products():
                settle("sw")
                step(nc.vector.tensor_tensor(sw_sq[:, :], sw[:, :], sw[:, :], ALU.mult), "sw_sq")
                step(nc.vector.tensor_tensor(sw_gamma[:, :], sw[:, :], lp[:, LC["bn2_gamma"]],
                                             ALU.mult), "sw_gamma")

            def norm0(b):
                normalise(0, b, t0[:, b, :], 2)


            def k_out(b):
                dve.wait_ge(k_mm, b + 1)
                nc.vector.tensor_scalar(k[:, b, :], k_ps, ep[:, EC["bk"]], None,
                                        ALU.add).then_inc(k_ready, 1)

            def row_max(b):
                dve.wait_ge(s_mm, b + 1)
                nc.vector.tensor_reduce(nmax[:, b, :],
                                        s_ps[b % 2][:, :].rearrange("p (a c) -> p a c", a=2),
                                        X_AXIS, ALU.max, negate=True).then_inc(nmax_ready, 1)

            def rinv_out(b):
                dve.wait_ge(exp_ready, 2 * b + 2)
                step(nc.vector.reciprocal(rinv[:, b, :], psum_rows[:, b, :]), "rinv", b)

            def x1_out(b):
                dve.wait_ge(o_mm, b + 1)
                dve.wait_ge(xb_ready, b + 1)
                settle("rinv", b)
                for par in range(2):
                    side = slice(par * HALF, (par + 1) * HALF)
                    nc.vector.scalar_tensor_tensor(
                        out=xs[1][:, b, side], in0=o_ps[:, side], scalar=rinv[:, b, par:par + 1],
                        in1=xb[:, b, side], op0=ALU.mult, op1=ALU.add).then_inc(x1_ready, 1)

            def x1_stats(b):
                dve.wait_ge(x1_ready, 2 * b + 2)
                gn_stats(1, b)

            def norm1(b):
                normalise(1, b, res[:, b, :], b + 1)

            def bn1_tuples(b):
                dve.wait_ge(rstd_ready[1], b + 1)
                halves = st[:, 1, b, :].rearrange("p (a f) -> p f a", a=2)
                nc.vector.tensor_scalar(halves[:, 1, :], halves[:, 1, :], gs[:, 1, b, 0:1],
                                        rstd[:, 1, b:b + 1], ALU.subtract, ALU.mult)
                step(nc.vector.tensor_scalar(halves[:, 2, :], halves[:, 2, :], rstd[:, 1, b:b + 1],
                                             rstd[:, 1, b:b + 1], ALU.mult, ALU.mult), "tuples", b)


            def bn1_aggr():
                settle("tuples", B - 1)
                step(nc.vector.bn_aggr(bn_mv[:, 0, :], st[:, 1, :, :].rearrange("p b f -> p (b f)")),
                     "bn_mv", 0)

            def bn1_var():
                settle("bn_mv", 0)
                nc.vector.tensor_scalar(bn_ve[:, 0:1], bn_mv[:, 0, 1:2], EPS, None,
                                        ALU.add).then_inc(bn_var_ready, 1)

            def bn_scale_out(i):
                dve.wait_ge(bn_rstd_ready, i + 1)
                if i == 1:
                    settle("sw_gamma")
                gamma = (lp[:, LC["bn1_gamma"]], sw_gamma[:, :])[i]
                step(nc.vector.tensor_tensor(bn_scale[:, i:i + 1], bn_rs[:, i:i + 1], gamma, ALU.mult),
                     "bn_scale", i)

            def bn_shift_out(i):
                settle("bn_scale", i)
                beta = lp[:, LC[("bn1_beta", "bn2_beta")[i]]]
                nc.vector.scalar_tensor_tensor(
                    out=bn_shift[:, i:i + 1], in0=bn_mv[:, i, 0:1], scalar=bn_scale[:, i:i + 1],
                    in1=beta, op0=ALU.mult, op1=ALU.subtract, reverse1=True).then_inc(bn_shift_ready, 1)

            def bn2_stats(b):
                dve.wait_ge(conv_mm, b + 1)
                nc.vector.bn_stats(bn2_st[:, b, :], conv_ps[b]).then_inc(bn2_st_ready, 1)

            def bn2_aggr():
                dve.wait_ge(bn2_st_ready, B)
                step(nc.vector.bn_aggr(bn_mv[:, 1, :], bn2_st[:, :, :].rearrange("p b f -> p (b f)")),
                     "bn_mv", 1)

            def bn2_var():
                settle("bn_mv", 1)
                settle("sw_sq")
                nc.vector.tensor_scalar(bn_ve[:, 1:2], bn_mv[:, 1, 1:2], sw_sq[:, :], EPS,
                                        ALU.mult, ALU.add).then_inc(bn_var_ready, 1)

            def h1_out(b):
                dve.wait_ge(bn2_out_ready, b + 1)
                nc.vector.tensor_tensor(h1[:, b, :], bn2_out[:, b, :], res[:, b, :],
                                        ALU.add).then_inc(h1_ready, 1)

            def x2_out(b):
                dve.wait_ge(h1_neg_ready, b + 1)
                dve.wait_ge(x1_h1_ready, b + 1)
                nc.vector.scalar_tensor_tensor(
                    out=xs[2][:, b, :], in0=h1_neg[:, b, :], scalar=one_minus_a[:, :],
                    in1=x1_h1[:, b, :], op0=ALU.mult, op1=ALU.add,
                    accum_out=mv[:, 2, b, 0:1]).then_inc(x2_ready, 1)


            def norm2(b):
                if b == 0:
                    settle("pad2")
                normalise(2, b, pad2[:, b, 1:H + 1, 1:W + 1], b + 1)

            def dw_tap(b, i):
                tap = PE_TAPS + i
                dy, dx = tap // 3, tap % 3
                dve.wait_ge(dw_acc_ready, (TAPS - PE_TAPS) * b + i)
                nc.vector.scalar_tensor_tensor(
                    out=dw_acc[:, b, i, :].rearrange("p (h w) -> p h w", h=H),
                    in0=pad2[:, b, dy:dy + H, dx:dx + W],
                    scalar=lp[:, LC["dw"].start + tap:LC["dw"].start + tap + 1],
                    in1=dw_acc[:, b, i - 1, :].rearrange("p (h w) -> p h w", h=H),
                    op0=ALU.mult, op1=ALU.add).then_inc(dw_acc_ready, 1)

            def dw_merge(b):
                dve.wait_ge(dw_acc_ready, (TAPS - PE_TAPS) * (b + 1))
                dve.wait_ge(dw_mm, b + 1)
                nc.vector.tensor_tensor(dw_sum[:, b, :], dw_ps[b], dw_acc[:, b, TAPS - PE_TAPS - 1, :],
                                        ALU.add).then_inc(dw_ready, 1)

            def prune1_max(b):
                dve.wait_ge(h2_ready, b + 1)
                step(nc.vector.tensor_reduce(amax[:, b, 0:1], h2[:, b, :], X_AXIS, ALU.max),
                     "amax", 0, b)

            def prune_keep(i, b):
                settle("amax", i, b)
                step(nc.vector.tensor_scalar(keep[:, b, i:i + 1], amax[:, b, i:i + 1],
                                             (DW_THRESH, PW_THRESH)[i], None, ALU.is_ge), "keep", i, b)

            def prune1_weights(b):
                settle("keep", 0, b)
                nc.vector.tensor_scalar(pwT_kept[:, b, :], lp[:, LC["pwT"]], keep[:, b, 0:1], None,
                                        ALU.mult).then_inc(pwT_ready, 1)

            def prune2_max(b):
                dve.wait_ge(y2_ready, b + 1)
                step(nc.vector.tensor_reduce(amax[:, b, 1:2], y2[:, b, :], X_AXIS, ALU.max),
                     "amax", 1, b)

            def x3_out(b):
                settle("keep", 1, b)
                nc.vector.scalar_tensor_tensor(
                    out=xs[3][:, b, :], in0=y2[:, b, :], scalar=keep[:, b, 1:2], in1=xs[2][:, b, :],
                    op0=ALU.mult, op1=ALU.add, accum_out=mv[:, 3, b, 0:1]).then_inc(x3_ready, 1)


            def norm3(b):
                normalise(3, b, t3[:, b, :], b + 1)

            def k3_max(b):
                dve.wait_ge(k3_mm, b + 1)
                nc.vector.tensor_reduce(nmax3[:, b:b + 1], k_ps, X_AXIS, ALU.max,
                                        negate=True).then_inc(nmax3_ready, 1)

            def rinv3_out(b):
                dve.wait_ge(e3_ready, b + 1)
                step(nc.vector.reciprocal(rinv3[:, b:b + 1], sum3[:, b:b + 1]), "rinv3", b)

            def context_out(b):
                dve.wait_ge(cx_mm, b + 1)
                if b == 0:
                    dve.wait_ge(masks, 1)
                nc.vector.tensor_tensor(ctxT[:, b, :], cx_ps, head_mask[:, :],
                                        ALU.mult).then_inc(cx_ready, 1)
    
            def project_out(b):
                dve.wait_ge(pj_mm, b + 1)
                settle("rinv3", b)
                nc.vector.tensor_scalar(proj[:, b, :], pj_ps, rinv3[:, b:b + 1], None,
                                        ALU.mult).then_inc(pj_ready, 1)

            def x4_out(b):
                dve.wait_ge(y3_mm, b + 1)
                nc.vector.scalar_tensor_tensor(out=xs[4][:, b, :], in0=y_ps,
                                               scalar=lp[:, LC["b_out"]], in1=xs[3][:, b, :],
                                               op0=ALU.add, op1=ALU.add).then_inc(x4_ready, 1)

            sw_stats()
            sw_aggr()
            sw_variance()
            k_out(0)
            sw_abs_sum()
            norm0(1)
            norm0(2)
            norm0(3)
            row_max(0)
            k_out(1)
            k_out(2)
            rinv_out(0)
            k_out(3)
            row_max(1)
            row_max(2)
            rinv_out(1)
            x1_out(0)
            x1_stats(0)
            rinv_out(2)
            gn_aggr(1, 0)
            row_max(3)
            gn_mean_sq(1, 0)
            sw_scale()
            sw_products()
            rinv_out(3)
            x1_out(1)
            group_out(1, 0)
            x1_stats(1)
            group_var(1, 0)
            gn_aggr(1, 1)
            gn_mean_sq(1, 1)
            x1_out(2)
            group_out(1, 1)
            x1_stats(2)
            group_var(1, 1)
            gn_aggr(1, 2)
            bn1_tuples(0)
            gn_mean_sq(1, 2)
            x1_out(3)
            bn1_tuples(1)
            x1_stats(3)
            norm1(0)
            gn_aggr(1, 3)
            group_out(1, 2)
            gn_mean_sq(1, 3)
            group_var(1, 2)
            norm1(1)
            group_out(1, 3)
            group_var(1, 3)
            bn1_tuples(2)
            norm1(2)
            bn1_tuples(3)
            norm1(3)
            bn1_aggr()
            bn1_var()
            bn_scale_out(0)
            bn_shift_out(0)
            bn2_stats(0)
            bn2_stats(1)
            bn2_stats(2)
            bn2_stats(3)
            bn2_aggr()
            bn2_var()
            bn_scale_out(1)
            bn_shift_out(1)
            h1_out(0)
            h1_out(1)
            h1_out(2)
            x2_out(0)
            x2_out(1)
            h1_out(3)
            x2_out(2)
            group_out(2, 0)
            group_var(2, 0)
            x2_out(3)
            group_out(2, 1)
            group_var(2, 1)
            norm2(0)
            group_out(2, 2)
            group_var(2, 2)
            norm2(1)
            dw_tap(0, 1)
            norm2(2)
            dw_tap(0, 2)
            dw_tap(0, 3)
            dw_merge(0)
            dw_tap(1, 1)
            dw_tap(1, 2)
            prune1_max(0)
            dw_tap(1, 3)
            prune_keep(0, 0)
            dw_merge(1)
            prune1_weights(0)
            dw_tap(2, 1)
            dw_tap(2, 2)
            prune1_max(1)
            dw_tap(2, 3)
            prune_keep(0, 1)
            group_out(2, 3)
            prune1_weights(1)
            group_var(2, 3)
            prune2_max(0)
            dw_merge(2)
            prune_keep(1, 0)
            norm2(3)
            x3_out(0)
            prune2_max(1)
            prune1_max(2)
            dw_tap(3, 1)
            prune_keep(0, 2)
            prune_keep(1, 1)
            prune1_weights(2)
            x3_out(1)
            dw_tap(3, 2)
            dw_tap(3, 3)
            group_out(3, 0)
            group_var(3, 0)
            prune2_max(2)
            dw_merge(3)
            prune_keep(1, 2)
            norm3(0)
            group_out(3, 1)
            x3_out(2)
            group_var(3, 1)
            prune1_max(3)
            prune_keep(0, 3)
            k3_max(0)
            prune1_weights(3)
            norm3(1)
            group_out(3, 2)
            group_var(3, 2)
            rinv3_out(0)
            norm3(2)
            k3_max(1)
            prune2_max(3)
            context_out(0)
            prune_keep(1, 3)
            rinv3_out(1)
            x3_out(3)
            k3_max(2)
            project_out(0)
            group_out(3, 3)
            group_var(3, 3)
            rinv3_out(2)
            x4_out(0)
            context_out(1)
            norm3(3)
            project_out(1)
            k3_max(3)
            x4_out(1)
            rinv3_out(3)
            context_out(2)
            project_out(2)
            context_out(3)
            x4_out(2)
            project_out(3)
            x4_out(3)
        @block.tensor
        def _(pe):
            def keep_warm(count):
                for _ in range(count):
                    nc.tensor.matmul(warm_ps[:, 0:N], warm[:, 0:C], warm[:, :],
                                     start=True, stop=True)

            last_in_bank7 = []

            def take_bank7(read, count):
                if last_in_bank7:
                    pe.wait_ge(*last_in_bank7.pop())
                last_in_bank7.append((read, count))

            def group_means(layer, b):
                if layer == 2 and b == 0:
                    pe.wait_ge(masks, 1)
                pe.wait_ge(stats_ready[layer], b + 1)
                take_bank7(group_read[layer], b + 1)
                nc.tensor.matmul(gn_ps[:, 0:2], (group_avg if layer < 2 else group_sum)[:, :],
                                 mv[:, layer, b, :], start=True, stop=True).then_inc(group_ready[layer], 1)

            def fold_weights():
                pe.wait_ge(early_in, 16)
                nc.tensor.matmul(setup_ps[:, 0:C], ep[:, EC["wv"]], ep[:, EC["woT"]],
                                 start=True, stop=True)

            def fold_bias():
                pe.wait_ge(pool_consts, 2)
                nc.tensor.matmul(setup_ps[:, C:2 * C], bias_rows[:, 0, :], ep[:, EC["woT"]],
                                 start=True, stop=False)
                nc.tensor.matmul(setup_ps[:, C:2 * C], bias_rows[:, 1, :], ident[:, :],
                                 start=False, stop=True).then_inc(setup_mm, 1)


            def project_q(b):
                pe.wait_ge(t_ready[0], b + 1)
                if b >= 1:
                    pe.wait_ge(q_ready, b)
                nc.tensor.matmul(q_ps, ep[:, EC["wqT"]], t0[:, b, :],
                                 start=True, stop=True).then_inc(q_mm, 1)

            def project_k(b):
                pe.wait_ge(t_ready[0], b + 1)
                if b >= 1:
                    pe.wait_ge(k_ready, b)
                nc.tensor.matmul(k_ps, ep[:, EC["wkT"]], t0[:, b, :],
                                 start=True, stop=True).then_inc(k_mm, 1)

            def project_v(b):
                pe.wait_ge(t_ready[0], b + 1)
                if b == 0:
                    pe.wait_ge(setup_done, 2)
                else:
                    pe.wait_ge(v_ready, b)
                for j in range(2):
                    ins = nc.tensor.matmul(v_ps[:, j * C:(j + 1) * C],
                                           t0[:, b, j * C:(j + 1) * C], woT_v,
                                           start=True, stop=True)
                ins.then_inc(v_mm, 1)

            def scores(b):
                pe.wait_ge(q_ready, b + 1)
                pe.wait_ge(k_ready, b + 1)
                if b >= 2:
                    pe.wait_ge(exp_ready, 2 * (b - 1))
                for par in range(2):
                    ins = nc.tensor.matmul(s_ps[b % 2][:, par * N:(par + 1) * N], q[:, b, par:N:2],
                                           k[:, b, :], start=True, stop=True)
                ins.then_inc(s_mm, 1)

            def transpose_prob(b):
                if b >= 1:
                    pe.wait_ge(pt_ready, b)
                for par in range(2):
                    pe.wait_ge(exp_ready, 2 * b + par + 1)
                    for j in range(2):
                        at = (2 * j + par) * C
                        ins = nc.tensor.transpose(pt_ps[:, at:at + C],
                                                  prob[:, b, par, j * C:(j + 1) * C], ident[:, :])
                ins.then_inc(pt_mm, 1)

            def attend(b):
                pe.wait_ge(v_ready, b + 1)
                pe.wait_ge(pt_ready, b + 1)
                if b >= 1:
                    pe.wait_ge(x1_ready, 2 * b)
                for par in range(2):
                    for j in range(2):
                        ins = nc.tensor.matmul(o_ps[:, par * C:(par + 1) * C],
                                               probT[:, b, j, par, :], vt[:, b, j, :],
                                               start=(j == 0), stop=(j == 1))
                ins.then_inc(o_mm, 1)


            def conv(b):
                if b == 0:
                    pe.wait_ge(conv_w_ready, 1)
                pe.wait_ge(sign_ready, b + 1)
                for tap in range(TAPS):
                    dy, dx = tap // 3, tap % 3
                    ins = nc.tensor.matmul(conv_ps[b], conv_w[:, tap, :],
                                           signs[:, b, dy:dy + H, dx:dx + W],
                                           start=(tap == 0), stop=(tap == TAPS - 1))
                ins.then_inc(conv_mm, 1)


            def depthwise(b):
                if b == 0:
                    pe.wait_ge(dw_diag_ready, 1)
                pe.wait_ge(t_ready[2], b + 1)
                if b >= 2:
                    pe.wait_ge(dw_ready, b - 1)
                for tap in range(PE_TAPS):
                    dy, dx = tap // 3, tap % 3
                    ins = nc.tensor.matmul(dw_ps[b], dw_diag[:, tap, :],
                                           pad2[:, b, dy:dy + H, dx:dx + W],
                                           start=(tap == 0), stop=(tap == PE_TAPS - 1))
                ins.then_inc(dw_mm, 1)

            def pointwise(b):
                pe.wait_ge(pwT_ready, b + 1)
                if b >= 1:
                    pe.wait_ge(y2_ready, b)
                nc.tensor.matmul(pw_ps, pwT_kept[:, b, :], h2[:, b, :],
                                 start=True, stop=True).then_inc(pw_mm, 1)

            wqkv = [lp[:, LC["wqkvT"].start + i * C:LC["wqkvT"].start + (i + 1) * C] for i in range(3)]

            def project_k3(b):
                pe.wait_ge(t_ready[3], b + 1)
                if b == 0:
                    pe.wait_ge(bn2_out_ready, B)
                else:
                    pe.wait_ge(e3_ready, b)
                nc.tensor.matmul(k_ps, wqkv[1], t3[:, b, :], start=True, stop=True).then_inc(k3_mm, 1)

            def project_q3(b):
                pe.wait_ge(t_ready[3], b + 1)
                if b == 0:
                    pe.wait_ge(bn2_out_ready, B)
                else:
                    pe.wait_ge(q3_ready, b)
                nc.tensor.matmul(q_ps, wqkv[0], t3[:, b, :], start=True, stop=True).then_inc(q3_mm, 1)

            def project_v3(b):
                pe.wait_ge(t_ready[3], b + 1)
                if b == 0:
                    pe.wait_ge(bn2_out_ready, B)
                else:
                    pe.wait_ge(kt3_ready, b)
                for j in range(2):
                    ins = nc.tensor.matmul(vt_ps[:, j * C:(j + 1) * C], t3[:, b, j * C:(j + 1) * C],
                                           wqkv[2], start=True, stop=True)
                ins.then_inc(vt3_mm, 1)

            def transpose_k(b):
                pe.wait_ge(vt3_ready, b + 1)
                pe.wait_ge(e3_ready, b + 1)
                for j in range(2):
                    ins = nc.tensor.transpose(kt_ps[:, j * C:(j + 1) * C],
                                              e3[:, b, j * C:(j + 1) * C], ident[:, :])
                ins.then_inc(kt3_mm, 1)

            def context(b):
                pe.wait_ge(kt3_ready, b + 1)
                take_bank7(cx_ready, b + 1)
                for j in range(2):
                    ins = nc.tensor.matmul(cx_ps, vt3[:, b, j, :], kt3[:, b, j, :],
                                           start=(j == 0), stop=(j == 1))
                ins.then_inc(cx_mm, 1)

            def project_context(b):
                pe.wait_ge(cx_ready, b + 1)
                if b == 0:
                    pe.wait_ge(bn2_out_ready, B)
                else:
                    pe.wait_ge(x4_ready, b)
                nc.tensor.matmul(pj_ps, ctxT[:, b, :], lp[:, LC["woutT"]],
                                 start=True, stop=True).then_inc(pj_mm, 1)

            def output(b):
                pe.wait_ge(q3_ready, b + 1)
                pe.wait_ge(pj_ready, b + 1)
                nc.tensor.matmul(y_ps, proj[:, b, :], q3[:, b, :],
                                 start=True, stop=True).then_inc(y3_mm, 1)

            pe.wait_ge(warm_ready, 1)
            keep_warm(14)
            pe.wait_ge(gn_consts, 1)
            group_means(0, 0)
            fold_weights()
            keep_warm(14)
            pe.wait_ge(stats_ready[0], 2)
            take_bank7(group_read[0], 2)
            nc.tensor.matmul(gn_ps[:, 0:2 * (B - 1)], group_avg[:, :],
                             mv[:, 0, 1:B, :].rearrange("p b f -> p (b f)"),
                             start=True, stop=True).then_inc(group_ready[0], 1)
            fold_bias()
            project_k(0)
            project_q(0)
            project_v(0)
            scores(0)
            project_k(1)
            project_v(1)
            project_q(1)
            project_k(2)
            transpose_prob(0)
            project_k(3)
            project_q(2)
            scores(1)
            scores(2)
            project_q(3)
            attend(0)
            transpose_prob(1)
            scores(3)
            project_v(2)
            transpose_prob(2)
            attend(1)
            project_v(3)
            group_means(1, 0)
            transpose_prob(3)
            attend(2)
            group_means(1, 1)
            attend(3)
            keep_warm(8)
            group_means(1, 2)
            group_means(1, 3)
            keep_warm(34)
            conv(0)
            conv(1)
            conv(2)
            conv(3)
            keep_warm(50)
            group_means(2, 0)
            keep_warm(4)
            group_means(2, 1)
            keep_warm(4)
            group_means(2, 2)
            depthwise(0)
            depthwise(1)
            depthwise(2)
            pointwise(0)
            group_means(2, 3)
            pointwise(1)
            depthwise(3)
            pointwise(2)
            group_means(3, 0)
            group_means(3, 1)
            project_v3(0)
            project_k3(0)
            project_q3(0)
            group_means(3, 2)
            pointwise(3)
            transpose_k(0)
            project_k3(1)
            project_q3(1)
            context(0)
            project_v3(1)
            project_q3(2)
            project_k3(2)
            project_context(0)
            transpose_k(1)
            group_means(3, 3)
            output(0)
            context(1)
            project_v3(2)
            project_context(1)
            project_k3(3)
            transpose_k(2)
            output(1)
            project_q3(3)
            project_v3(3)
            context(2)
            transpose_k(3)
            project_context(2)
            context(3)
            output(2)
            project_context(3)
            output(3)


def kernel(**inputs):
    import numpy as np
    import concourse.bacc as bacc
    from concourse.bass_utils import run_bass_kernel_spmd

    def arr(name):
        return np.ascontiguousarray(np.asarray(inputs[name]))

    def col(*names):
        return np.stack([arr(n) for n in names], axis=1)

    conv = arr("L1_conv_conv_w").reshape(C // CONV_GROUP, CONV_GROUP, CONV_GROUP, TAPS)
    early = [arr("L0_conv_Wq").T, arr("L0_conv_Wk").T, arr("L0_conv_Wv"), arr("L0_conv_Wo").T,
             col("L0_conv_bq", "L0_conv_bk", "L0_conv_bv", "L0_conv_bo")]
    late = [conv.transpose(0, 2, 3, 1).reshape(C, TAPS * CONV_GROUP),
            arr("L1_conv_conv_w").reshape(C, CONV_FAN), arr("L2_conv_dw_w").reshape(C, TAPS),
            col("L1_conv_bn1_gamma", "L1_conv_bn1_beta", "L1_conv_bn2_gamma", "L1_conv_bn2_beta",
                "L1_conv_prelu_a", "L2_conv_dw_b", "L2_conv_pw_b", "L2_conv_bn1_g", "L2_conv_bn2_g",
                "L2_conv_bn1_b", "L2_conv_bn2_b", "L2_conv_bn1_m", "L2_conv_bn2_m", "L2_conv_bn1_v",
                "L2_conv_bn2_v", "L3_conv_b_out"),
            arr("L2_conv_pw_w").reshape(C, C).T, arr("L3_conv_w_qkv").T, arr("L3_conv_w_out").T]
    arrays = {"x": arr("x"), "early": np.ascontiguousarray(np.concatenate(early, axis=1)),
              "late": np.ascontiguousarray(np.concatenate(late, axis=1))}

    nc = bacc.Bacc("TRN2", target_bir_lowering=False, num_devices=1)
    args = [nc.dram_tensor(f"in_{name}", a.shape, mybir.dt.float32, kind="ExternalInput").ap()
            for name, a in arrays.items()]
    out = nc.dram_tensor("out", (B, C, H, W), mybir.dt.float32, kind="ExternalOutput").ap()
    build(nc, *args, out)
    r = run_bass_kernel_spmd(nc, [{f"in_{name}": a for name, a in arrays.items()}], core_ids=[0])
    return r.results[0]["out"]
```

```python
import concourse.bass as bass
from concourse import mybir
from contextlib import ExitStack

B, C, H, W = 4, 128, 16, 16
N = H * W
HALF = N // 2
TAPS = 9
PH, PW = H + 2, W + 2
GN_GROUP = C // 32
CONV_GROUP = C // 16
HEAD = 16
CONV_FAN = CONV_GROUP * TAPS
EPS = 1e-5
PE_TAPS, ACT_TAPS = 5, 2
DVE_TAPS = TAPS - PE_TAPS - ACT_TAPS
DW_THRESH = 4.0
PW_THRESH = 0.001

EARLY = [("wqT", C), ("wkT", C), ("wv", C), ("woT", C), ("bq", 1), ("bk", 1), ("bv", 1), ("bo", 1)]
LATE = [("conv_in", TAPS * CONV_GROUP), ("conv_out", CONV_FAN), ("dw", TAPS),
        ("bn1_gamma", 1), ("bn1_beta", 1), ("bn2_gamma", 1), ("bn2_beta", 1), ("prelu", 1),
        ("l2_bias", 2), ("l2_g", 2), ("l2_b", 2), ("l2_m", 2), ("l2_v", 2), ("b_out", 1),
        ("pwT", C), ("wqkvT", 3 * C), ("woutT", C)]


def columns(fields):
    at, out = 0, {}
    for name, width in fields:
        out[name] = slice(at, at + width)
        at += width
    return out, at


def build(nc, x, early, late, out):
    fp32, bf16 = mybir.dt.float32, mybir.dt.bfloat16
    ALU = mybir.AluOpType
    ACT = mybir.ActivationFunctionType
    X_AXIS = mybir.AxisListType.X
    EC, EARLY_W = columns(EARLY)
    LC, LATE_W = columns(LATE)
    x_v = x.rearrange("b c h w -> b c (h w)")
    out_v = out.rearrange("b c h w -> b c (h w)")

    ctx = ExitStack()
    with ctx:
        def sb(name, shape, dt=fp32):
            return ctx.enter_context(nc.sbuf_tensor(name, shape, dt))

        def sem(name):
            return ctx.enter_context(nc.semaphore(name))

        ep = sb("early_params", [C, EARLY_W])
        lp = sb("late_params", [C, LATE_W])
        ident = sb("ident", [C, C])
        warm = sb("warm", [C, N], bf16)
        ones = sb("ones", [C, C])
        group_avg = sb("group_avg", [C, C])
        group_sum = sb("group_sum", [C, C])
        head_mask = sb("head_mask", [C, C])
        conv_mask = sb("conv_mask", [C, C // CONV_GROUP], bf16)
        eps_row = sb("eps_row", [C, 2])
        minus_half = sb("minus_half", [C, B])
        bias_rows = sb("bias_rows", [C, 2, C])
        setup = sb("setup", [C, 2, C])
        woT_v = setup[:, 0, :]
        v_bias = setup[:, 1, :]
        bq_s = sb("bq_scaled", [C, 1])
        conv_sign = sb("conv_sign", [C, TAPS, CONV_GROUP], bf16)
        conv_w = sb("conv_blocks", [C, TAPS, C], bf16)
        dw_diag = sb("dw_diag", [C, TAPS, C])
        valid = sb("valid", [C, PH, PW])
        valid_sum = sb("valid_sum", [C, N])
        sw_st = sb("sw_stats", [C, 6])
        sw_mv = sb("sw_mean_var", [C, 2])
        sw_dev = sb("sw_deviation", [C, CONV_FAN])
        sw_abs = sb("sw_abs_sum", [C, 1])
        sw_var = sb("sw_var", [C, 1])
        sw_rstd = sb("sw_rstd", [C, 1])
        sw = sb("sw", [C, 1])
        sw_sq = sb("sw_squared", [C, 1])
        sw_gamma = sb("sw_gamma", [C, 1])
        l2_ve = sb("l2_var_eps", [C, 2])
        l2_rs = sb("l2_rstd", [C, 2])
        l2_scale = sb("l2_scale", [C, 2])
        l2_t = sb("l2_t", [C, 2])
        l2_t2 = sb("l2_t2", [C, 2])
        l2_shift = sb("l2_shift", [C, 2])

        xs = [sb(f"x{i}", [C, B, N] if i != 2 else [C, B, PH, PW]) for i in range(5)]
        x2_inside = xs[2][:, :, 1:H + 1, 1:W + 1]
        xb = sb("x_bias", [C, B, N])
        t0 = sb("t0", [C, B, N])
        res = sb("res", [C, B, N])
        t3 = sb("t3", [C, B, N])
        signs = sb("signs", [C, B, PH, PW], bf16)
        q = sb("q", [C, B, N])
        k = sb("k", [C, B, N])
        vt = sb("vt", [C, B, 2, C])
        nmax = sb("nmax", [C, B, 2])
        prob = sb("prob", [C, B, 2, N])
        psum_rows = sb("prob_sum", [C, B, 2])
        rinv = sb("rinv", [C, B, 2])
        probT = sb("probT", [C, B, 2, 2, C])
        x1_res = sb("x1_res", [C, B, N])
        bn2_out = sb("bn2_out", [C, B, N])
        h1 = sb("h1", [C, B, N])
        x1_h1 = sb("x1_h1", [C, B, N])
        h1_neg = sb("h1_neg", [C, B, N])
        one_minus_a = sb("one_minus_a", [C, 1])
        act_taps = sb("act_taps", [C, B, ACT_TAPS, N])
        act_sum = sb("act_sum", [C, B, N])
        dw_acc = sb("dw_acc", [C, B, DVE_TAPS, N])
        mean_taps = sb("mean_taps", [C, B, N])
        dw_rest = sb("dw_rest", [C, B, N])
        dw_sum = sb("dw_sum", [C, B, N])
        dw_scale = sb("dw_scale", [C, B])
        h2 = sb("h2", [C, B, N])
        amax = sb("amax", [C, B, 2])
        keep = sb("keep", [C, B])
        pwT_kept = sb("pwT_kept", [C, B, C])
        y2 = sb("y2", [C, B, N])
        q3 = sb("q3", [C, B, N])
        nmax3 = sb("nmax3", [C, B])
        e3 = sb("e3", [C, B, N])
        sum3 = sb("sum3", [C, B])
        rinv3 = sb("rinv3", [C, B])
        vt3 = sb("vt3", [C, B, 2, C])
        kt3 = sb("kt3", [C, B, 2, C])
        ctxT = sb("ctxT", [C, B, C])
        proj = sb("proj", [C, B, C])

        st = sb("gn_stats", [C, 4, B, 6])
        mv = sb("gn_mean_sq", [C, 4, B, 3])
        msq0 = sb("gn_mean_squared", [C, B])
        squares = sb("squares", [C, 2, B, N])
        gs = sb("gn_group", [C, 4, B, 2])
        ve = sb("gn_var_eps", [C, 4, B])
        rstd = sb("gn_rstd", [C, 4, B])
        bn1_dev = sb("bn1_deviation", [C, B])
        bn1_dev_sq = sb("bn1_deviation_sq", [C, B])
        bn1_sq = sb("bn1_mean_sq", [C, B])
        bn1_inv = sb("bn1_inv_var", [C, B])
        bn1_tmp = sb("bn1_products", [C, 2, B])
        bn1_e2 = sb("bn1_e2", [C, 2])
        bn_mv = sb("bn_mean_var", [C, 2, 2])
        bn_ve = sb("bn_var_eps", [C, 2])
        bn_rs = sb("bn_rstd", [C, 2])
        bn_scale = sb("bn_scale", [C, 2])
        bn_shift = sb("bn_shift", [C, 2])
        bn2_st = sb("bn2_stats", [C, B, 6])

        banks = [ctx.enter_context(nc.psum_tensor(f"bank{i}", [C, 512], fp32)) for i in range(8)]

        q_ps, k_ps = banks[0][:, 0:N], banks[1][:, 0:N]
        v_ps = banks[2][:, 0:N]
        s_ps = [banks[3], banks[4]]
        valid_ps = banks[3][:, 0:N]
        pt_ps = banks[5]
        o_ps = [banks[i][:, 0:N] for i in (6, 6, 6, 1)]
        setup_ps = banks[6]
        warm_ps = banks[4]
        conv_ps = [banks[i][:, 0:N] for i in (0, 1, 2, 5)]
        dw_ps = [banks[3 + b % 2][:, 0:N] for b in range(B)]
        pw_ps = banks[6][:, 0:N]
        k3_ps = [banks[(1, 4)[b % 2]][:, 0:N] for b in range(B)]
        vt_ps = banks[3][:, 0:N]
        kt_ps = banks[5][:, 0:N]
        pj_ps = banks[6][:, 0:C]
        y_ps = banks[2][:, 0:N]
        gn_ps = banks[7]
        cx_ps = banks[7][:, 0:C]

        x_in = [sem("x_in0"), sem("x_in1")]
        early_in = sem("early_in")
        late_in = sem("late_in")
        stored = sem("stored")
        pool_step = sem("pool_step")
        dve_step = sem("dve_step")
        warm_ready = sem("warm_ready")
        gn_consts = sem("gn_consts")
        pool_consts = sem("pool_consts")
        sum_masks = sem("sum_masks")
        head_mask_ready = sem("head_mask_ready")
        conv_w_ready = sem("conv_w_ready")
        dw_diag_ready = sem("dw_diag_ready")
        valid_mm, valid_ready = sem("valid_mm"), sem("valid_ready")
        l2_consts = sem("l2_consts")
        borders = sem("borders")
        conv_sign_ready = sem("conv_sign_ready")
        setup_mm = sem("setup_mm")
        setup_done = sem("setup_done")
        sw_var_ready = sem("sw_var_ready")
        sw_rstd_ready = sem("sw_rstd_ready")
        stats_ready = [sem(f"stats_ready{i}") for i in range(4)]
        group_ready = [sem(f"group_ready{i}") for i in range(4)]
        group_read = [sem(f"group_read{i}") for i in range(4)]
        var_ready = [sem(f"var_ready{i}") for i in range(4)]
        rstd_ready = [sem(f"rstd_ready{i}") for i in range(4)]
        t_ready = [sem(f"t_ready{i}") for i in range(4)]
        q_mm, k_mm, v_mm = sem("q_mm"), sem("k_mm"), sem("v_mm")
        q_ready, k_ready, v_ready = sem("q_ready"), sem("k_ready"), sem("v_ready")
        s_mm = sem("s_mm")
        nmax_ready = sem("nmax_ready")
        exp_ready = sem("exp_ready")
        pt_mm, pt_ready = sem("pt_mm"), sem("pt_ready")
        o_mm = sem("o_mm")
        xb_ready = sem("xb_ready")
        x1_ready = sem("x1_ready")
        bn_var_ready, bn_rstd_ready = sem("bn_var_ready"), sem("bn_rstd_ready")
        bn_shift_ready = sem("bn_shift_ready")
        sign_ready = sem("sign_ready")
        conv_mm = sem("conv_mm")
        bn2_st_ready = sem("bn2_st_ready")
        bn2_out_ready = sem("bn2_out_ready")
        h1_ready = sem("h1_ready")
        h1_neg_ready = sem("h1_neg_ready")
        x1_h1_ready = sem("x1_h1_ready")
        x2_ready = sem("x2_ready")
        dw_mm = sem("dw_mm")
        act_tap_ready = [sem(f"act_tap_ready{i}") for i in range(ACT_TAPS)]
        act_sum_ready = sem("act_sum_ready")
        dw_acc_ready = sem("dw_acc_ready")
        mean_taps_ready = sem("mean_taps_ready")
        dw_rest_ready = sem("dw_rest_ready")
        dw_sum_ready = sem("dw_sum_ready")
        dw_scale_ready = sem("dw_scale_ready")
        h2_ready = sem("h2_ready")
        pwT_ready = sem("pwT_ready")
        pw_mm = sem("pw_mm")
        y2_ready = sem("y2_ready")
        x3_ready = sem("x3_ready")
        k3_mm, q3_mm, vt3_mm = sem("k3_mm"), sem("q3_mm"), sem("vt3_mm")
        nmax3_ready, rinv3_ready = sem("nmax3_ready"), sem("rinv3_ready")
        q3_ready, e3_ready, vt3_ready = sem("q3_ready"), sem("e3_ready"), sem("vt3_ready")
        kt3_mm, kt3_ready = sem("kt3_mm"), sem("kt3_ready")
        cx_mm, cx_ready = sem("cx_mm"), sem("cx_ready")
        pj_mm, pj_ready = sem("pj_mm"), sem("pj_ready")
        y3_mm = sem("y3_mm")
        x4_ready = sem("x4_ready")

        SCALE = float(C) ** -0.5

        block = ctx.enter_context(nc.Block())

        @block.sync
        def _(sp):
            sp.dma_start(xs[0][:, 0, :], x_v[0]).then_inc(x_in[0], 16)
            sp.dma_start(xs[0][:, 1:B, :], x_v[1:B].rearrange("b c n -> c b n")).then_inc(x_in[1], 16)
            sp.dma_start(ep[:, :], early).then_inc(early_in, 16)
            sp.dma_start(lp[:, :], late).then_inc(late_in, 16)
            for b in range(B):
                sp.wait_ge(x4_ready, b + 1)
                sp.dma_start(out_v[b], xs[4][:, b, :]).then_inc(stored, 16)
            sp.wait_ge(stored, 16 * B)

        @block.gpsimd
        def _(pool):
            steps = [0]

            def step(ins):
                steps[0] += 1
                ins.then_inc(pool_step, 1)
                pool.wait_ge(pool_step, steps[0])

            def same_block(tile, size):
                inner = [[0, size]] if tile.shape[1] == C else []
                step(nc.gpsimd.affine_select(out=tile[:, :], in_=tile[:, :], compare_op=ALU.is_ge,
                                             fill=0.0, base=0, pattern=[[-size, C // size]] + inner,
                                             channel_multiplier=1))
                return nc.gpsimd.affine_select(out=tile[:, :], in_=tile[:, :], compare_op=ALU.is_ge,
                                               fill=0.0, base=size - 1,
                                               pattern=[[size, C // size]] + inner,
                                               channel_multiplier=-1)

            nc.gpsimd.memset(warm[:, :], 1.0).then_inc(warm_ready, 1)
            nc.gpsimd.memset(ones[:, :], 1.0)
            nc.gpsimd.memset(eps_row[:, 0:1], 0.0)
            nc.gpsimd.memset(eps_row[:, 1:2], EPS)
            nc.gpsimd.memset(minus_half[:, :], -0.5)
            step(nc.gpsimd.memset(group_avg[:, :], 1.0 / GN_GROUP))
            same_block(group_avg, GN_GROUP).then_inc(gn_consts, 1)
            step(nc.gpsimd.memset(ident[:, :], 0.0))
            nc.gpsimd.affine_select(out=ident[:, :], in_=ident[:, :], compare_op=ALU.not_equal,
                                    fill=1.0, base=0, pattern=[[-1, C]],
                                    channel_multiplier=1).then_inc(pool_consts, 1)

            def root(out_ap, in_ap):
                n = in_ap.shape[1]
                return nc.gpsimd.tensor_tensor(out_ap, in_ap, minus_half[:, 0:n], ALU.pow)

            pool.wait_ge(var_ready[0], 1)
            root(rstd[:, 0, 0:1], ve[:, 0, 0:1]).then_inc(rstd_ready[0], 1)
            pool.wait_ge(early_in, 16)
            for i, name in enumerate(("bv", "bo")):
                ins = nc.gpsimd.tensor_scalar(bias_rows[:, i, :], ones[:, :], ep[:, EC[name]], 0.0,
                                              ALU.mult, ALU.add)
            ins.then_inc(pool_consts, 1)

            def other_roots():
                pool.wait_ge(var_ready[0], 2)
                root(rstd[:, 0, 1:B], ve[:, 0, 1:B]).then_inc(rstd_ready[0], 1)

            def x_bias(b):
                pool.wait_ge(setup_done, 2)
                pool.wait_ge(x_in[min(b, 1)], 16)
                nc.gpsimd.tensor_tensor(xb[:, b, :].rearrange("p (a c) -> p a c", a=2),
                                        xs[0][:, b, :].rearrange("p (a c) -> p a c", a=2),
                                        v_bias.unsqueeze(1).to_broadcast([C, 2, C]),
                                        ALU.add).then_inc(xb_ready, 1)

            def conv_weights():
                step(nc.gpsimd.memset(conv_mask[:, :], 1.0))
                step(same_block(conv_mask, CONV_GROUP))
                pool.wait_ge(conv_sign_ready, 1)
                groups = C // CONV_GROUP
                for tap in range(TAPS):
                    ins = nc.gpsimd.tensor_tensor(
                        conv_w[:, tap, :].rearrange("p (g o) -> p g o", o=CONV_GROUP),
                        conv_sign[:, tap, :].unsqueeze(1).to_broadcast([C, groups, CONV_GROUP]),
                        conv_mask[:, :].unsqueeze(2).to_broadcast([C, groups, CONV_GROUP]), ALU.mult)
                ins.then_inc(conv_w_ready, 1)

            def sw_root():
                pool.wait_ge(sw_var_ready, 1)
                root(sw_rstd[:, :], sw_var[:, :]).then_inc(sw_rstd_ready, 1)

            def l2_constants():
                pool.wait_ge(late_in, 16)
                step(nc.gpsimd.tensor_scalar(l2_ve[:, :], lp[:, LC["l2_v"]], 1.0, EPS, ALU.mult, ALU.add))
                step(root(l2_rs[:, :], l2_ve[:, :]))
                nc.gpsimd.tensor_tensor(l2_t[:, :], lp[:, LC["l2_bias"]], lp[:, LC["l2_m"]], ALU.subtract)
                step(nc.gpsimd.tensor_tensor(l2_scale[:, :], l2_rs[:, :], lp[:, LC["l2_g"]], ALU.mult))
                step(nc.gpsimd.tensor_tensor(l2_t2[:, :], l2_t[:, :], l2_scale[:, :], ALU.mult))
                nc.gpsimd.tensor_tensor(l2_shift[:, :], l2_t2[:, :], lp[:, LC["l2_b"]],
                                        ALU.add).then_inc(l2_consts, 1)

            def valid_mask():
                step(nc.gpsimd.memset(valid[:, :, :], 0.0))
                nc.gpsimd.memset(valid[:, 1:H + 1, 1:W + 1], 1.0)
                nc.gpsimd.tensor_scalar(group_sum[:, :], group_avg[:, :], 1.0 / N, 0.0,
                                        ALU.mult, ALU.add).then_inc(sum_masks, 1)

            def head_masks():
                step(nc.gpsimd.memset(head_mask[:, :], 1.0))
                same_block(head_mask, HEAD).then_inc(head_mask_ready, 1)

            def gn_root(layer, b):
                pool.wait_ge(var_ready[layer], b + 1)
                root(rstd[:, layer, b:b + 1], ve[:, layer, b:b + 1]).then_inc(rstd_ready[layer], 1)

            def sum_act_taps(b):
                for i in range(ACT_TAPS):
                    pool.wait_ge(act_tap_ready[i], b + 1)
                nc.gpsimd.tensor_tensor(act_sum[:, b, :], act_taps[:, b, 0, :], act_taps[:, b, 1, :],
                                        ALU.add).then_inc(act_sum_ready, 1)

            def less_mean(b):
                pool.wait_ge(dw_acc_ready, b + 1)
                pool.wait_ge(mean_taps_ready, b + 1)
                nc.gpsimd.tensor_tensor(dw_rest[:, b, :], dw_acc[:, b, DVE_TAPS - 1, :],
                                        mean_taps[:, b, :], ALU.subtract).then_inc(dw_rest_ready, 1)

            def dw_scale_out(b):
                pool.wait_ge(rstd_ready[2], b + 1)
                nc.gpsimd.tensor_tensor(dw_scale[:, b:b + 1], rstd[:, 2, b:b + 1], l2_scale[:, 0:1],
                                        ALU.mult).then_inc(dw_scale_ready, 1)

            def bn_root(i):
                pool.wait_ge(bn_var_ready, i + 1)
                root(bn_rs[:, i:i + 1], bn_ve[:, i:i + 1]).then_inc(bn_rstd_ready, 1)

            def x1_res_out(b):
                pool.wait_ge(t_ready[1], b + 1)
                steps[0] += 1
                nc.gpsimd.tensor_tensor(x1_res[:, b, :], xs[1][:, b, :], res[:, b, :],
                                        ALU.add).then_inc(pool_step, 1)

            def x1_h1_out(b):
                pool.wait_ge(bn2_out_ready, b + 1)
                pool.wait_ge(pool_step, steps[0])
                nc.gpsimd.tensor_tensor(x1_h1[:, b, :], bn2_out[:, b, :], x1_res[:, b, :],
                                        ALU.add).then_inc(x1_h1_ready, 1)

            valid_mask()
            head_masks()
            other_roots()
            x_bias(0)
            x_bias(1)
            x_bias(2)
            x_bias(3)
            l2_constants()
            conv_weights()
            sw_root()
            gn_root(1, 0)
            x1_res_out(0)
            gn_root(1, 1)
            gn_root(1, 2)
            gn_root(1, 3)
            x1_res_out(1)
            bn_root(0)
            x1_res_out(2)
            x1_res_out(3)
            bn_root(1)
            x1_h1_out(0)
            x1_h1_out(1)
            x1_h1_out(2)
            x1_h1_out(3)
            sum_act_taps(0)
            sum_act_taps(1)
            gn_root(2, 0)
            dw_scale_out(0)
            less_mean(0)
            sum_act_taps(2)
            less_mean(1)
            gn_root(2, 1)
            sum_act_taps(3)
            dw_scale_out(1)
            less_mean(2)
            gn_root(2, 2)
            less_mean(3)
            dw_scale_out(2)
            gn_root(2, 3)
            dw_scale_out(3)
            gn_root(3, 0)
            gn_root(3, 1)
            gn_root(3, 2)
            gn_root(3, 3)
        @block.scalar
        def _(act):
            act.wait_ge(early_in, 16)
            nc.scalar.activation(bq_s[:, :], ep[:, EC["bq"]], ACT.Copy, scale=SCALE).then_inc(setup_done, 1)
            act.wait_ge(late_in, 16)
            nc.scalar.activation(conv_sign[:, :, :],
                                 lp[:, LC["conv_in"]].rearrange("p (t o) -> p t o", t=TAPS),
                                 ACT.Sign).then_inc(conv_sign_ready, 1)

            def setup_out():
                act.wait_ge(setup_mm, 1)
                nc.scalar.activation(setup[:, :, :].rearrange("p a c -> p (a c)"), setup_ps[:, 0:2 * C],
                                     ACT.Copy).then_inc(setup_done, 1)

            def dw_diagonal(tap):
                if tap == 0:
                    act.wait_ge(pool_consts, 1)
                at = LC["dw"].start + tap
                nc.scalar.activation(dw_diag[:, tap, :], ident[:, :], ACT.Copy,
                                     scale=lp[:, at:at + 1]).then_inc(dw_diag_ready, 1)

            def valid_taps_out():
                act.wait_ge(valid_mm, 1)
                nc.scalar.activation(valid_sum[:, :], valid_ps, ACT.Copy).then_inc(valid_ready, 1)

            def q_out(b):
                act.wait_ge(q_mm, b + 1)
                nc.scalar.activation(q[:, b, :], q_ps, ACT.Identity,
                                     bias=bq_s[:, :], scale=SCALE).then_inc(q_ready, 1)

            def softmax(b):
                act.wait_ge(nmax_ready, b + 1)
                for par in range(2):
                    nc.scalar.activation(prob[:, b, par, :], s_ps[b % 2][:, par * N:(par + 1) * N],
                                         ACT.Exp, bias=nmax[:, b, par:par + 1],
                                         accum_out=psum_rows[:, b, par:par + 1]).then_inc(exp_ready, 1)

            def v_out(b):
                act.wait_ge(v_mm, b + 1)
                nc.scalar.activation(vt[:, b, :, :].rearrange("p a c -> p (a c)"), v_ps,
                                     ACT.Copy).then_inc(v_ready, 1)

            def prob_out(b):
                act.wait_ge(pt_mm, b + 1)
                nc.scalar.activation(probT[:, b, :, :, :].rearrange("p j a c -> p (j a c)"),
                                     pt_ps[:, :], ACT.Copy).then_inc(pt_ready, 1)

            def sign_out(b):
                if b == 0:
                    act.wait_ge(borders, 1)
                    act.wait_ge(bn_shift_ready, 1)
                act.wait_ge(t_ready[1], b + 1)
                nc.scalar.activation(signs[:, b, 1:H + 1, 1:W + 1],
                                     res[:, b, :].rearrange("p (h w) -> p h w", h=H), ACT.Sign,
                                     bias=bn_shift[:, 0:1], scale=bn_scale[:, 0:1]).then_inc(sign_ready, 1)

            def bn2_apply(b):
                if b == 0:
                    act.wait_ge(bn_shift_ready, 2)
                nc.scalar.activation(bn2_out[:, b, :], conv_ps[b], ACT.Identity,
                                     bias=bn_shift[:, 1:2],
                                     scale=bn_scale[:, 1:2]).then_inc(bn2_out_ready, 1)

            def negative_part(b):
                act.wait_ge(h1_ready, b + 1)
                nc.scalar.activation(h1_neg[:, b, :], h1[:, b, :], ACT.Relu,
                                     scale=-1.0).then_inc(h1_neg_ready, 1)

            def square_sum(layer, b):
                act.wait_ge(x2_ready if layer == 2 else x3_ready, b + 1)
                out, src = squares[:, layer - 2, b, :], xs[3][:, b, :]
                if layer == 2:
                    out, src = out.rearrange("p (h w) -> p h w", h=H), x2_inside[:, b]
                nc.scalar.activation(out, src, ACT.Square,
                                     accum_out=mv[:, layer, b, 2:3]).then_inc(stats_ready[layer], 1)

            def act_tap(b, i):
                act.wait_ge(x2_ready, b + 1)
                tap = PE_TAPS + i
                dy, dx = tap // 3, tap % 3
                nc.scalar.activation(
                    act_taps[:, b, i, :].rearrange("p (h w) -> p h w", h=H),
                    xs[2][:, b, dy:dy + H, dx:dx + W], ACT.Copy,
                    scale=lp[:, LC["dw"].start + tap:LC["dw"].start + tap + 1]
                ).then_inc(act_tap_ready[i], 1)

            def mean_taps_out(b):
                if b == 0:
                    act.wait_ge(valid_ready, 1)
                act.wait_ge(group_read[2], b + 1)
                nc.scalar.activation(mean_taps[:, b, :], valid_sum[:, :], ACT.Copy,
                                     scale=gs[:, 2, b, 0:1]).then_inc(mean_taps_ready, 1)

            def relu1(b):
                if b == 0:
                    act.wait_ge(l2_consts, 1)
                act.wait_ge(dw_sum_ready, b + 1)
                act.wait_ge(dw_scale_ready, b + 1)
                nc.scalar.activation(h2[:, b, :], dw_sum[:, b, :], ACT.Relu, bias=l2_shift[:, 0:1],
                                     scale=dw_scale[:, b:b + 1]).then_inc(h2_ready, 1)

            def relu2(b):
                act.wait_ge(pw_mm, b + 1)
                nc.scalar.activation(y2[:, b, :], pw_ps, ACT.Relu, bias=l2_shift[:, 1:2],
                                     scale=l2_scale[:, 1:2]).then_inc(y2_ready, 1)

            def softmax3(b):
                act.wait_ge(nmax3_ready, b + 1)
                nc.scalar.activation(e3[:, b, :], k3_ps[b], ACT.Exp, bias=nmax3[:, b:b + 1],
                                     accum_out=sum3[:, b:b + 1]).then_inc(e3_ready, 1)

            def q3_out(b):
                act.wait_ge(q3_mm, b + 1)
                nc.scalar.activation(q3[:, b, :], q_ps, ACT.Copy).then_inc(q3_ready, 1)

            def v3_out(b):
                act.wait_ge(vt3_mm, b + 1)
                nc.scalar.activation(vt3[:, b, :, :].rearrange("p a c -> p (a c)"), vt_ps,
                                     ACT.Copy).then_inc(vt3_ready, 1)

            def kt3_out(b):
                act.wait_ge(kt3_mm, b + 1)
                nc.scalar.activation(kt3[:, b, :, :].rearrange("p a c -> p (a c)"), kt_ps,
                                     ACT.Copy).then_inc(kt3_ready, 1)

            def project_out(b):
                act.wait_ge(pj_mm, b + 1)
                act.wait_ge(rinv3_ready, b + 1)
                nc.scalar.activation(proj[:, b, :], pj_ps, ACT.Copy,
                                     scale=rinv3[:, b:b + 1]).then_inc(pj_ready, 1)

            act.wait_ge(setup_done, 1)
            dw_diagonal(0)
            dw_diagonal(1)
            dw_diagonal(2)
            dw_diagonal(3)
            q_out(0)
            dw_diagonal(4)
            dw_diagonal(5)
            dw_diagonal(6)
            setup_out()
            dw_diagonal(7)
            dw_diagonal(8)
            v_out(0)
            q_out(1)
            softmax(0)
            q_out(2)
            v_out(1)
            q_out(3)
            softmax(1)
            prob_out(0)
            softmax(2)
            prob_out(1)
            softmax(3)
            prob_out(2)
            v_out(2)
            v_out(3)
            prob_out(3)
            sign_out(0)
            valid_taps_out()
            sign_out(1)
            sign_out(2)
            sign_out(3)
            bn2_apply(0)
            bn2_apply(1)
            bn2_apply(2)
            negative_part(0)
            negative_part(1)
            negative_part(2)
            bn2_apply(3)
            square_sum(2, 0)
            act_tap(0, 0)
            act_tap(1, 0)
            act_tap(0, 1)
            act_tap(1, 1)
            negative_part(3)
            square_sum(2, 1)
            square_sum(2, 2)
            act_tap(2, 0)
            mean_taps_out(0)
            act_tap(3, 0)
            act_tap(2, 1)
            square_sum(2, 3)
            mean_taps_out(1)
            act_tap(3, 1)
            mean_taps_out(2)
            relu1(0)
            relu1(1)
            mean_taps_out(3)
            relu2(0)
            relu1(2)
            square_sum(3, 0)
            relu2(1)
            relu1(3)
            relu2(2)
            square_sum(3, 1)
            relu2(3)
            square_sum(3, 2)
            v3_out(0)
            softmax3(0)
            q3_out(0)
            square_sum(3, 3)
            softmax3(1)
            kt3_out(0)
            q3_out(1)
            v3_out(1)
            kt3_out(1)
            softmax3(2)
            q3_out(2)
            v3_out(2)
            project_out(0)
            softmax3(3)
            kt3_out(2)
            project_out(1)
            v3_out(3)
            kt3_out(3)
            project_out(2)
            q3_out(3)
            project_out(3)
        @block.vector
        def _(dve):
            steps = [0]
            made = {}

            def square(image):
                return image.rearrange("p (h w) -> p h w", h=H)

            def step(ins, *name):
                steps[0] += 1
                made[name] = steps[0]
                ins.then_inc(dve_step, 1)

            def settle(*name):
                dve.wait_ge(dve_step, made[name])

            nc.vector.memset(signs[:, :, :, :].rearrange("p b h w -> p (b h w)").bitcast(fp32),
                             0.0).then_inc(borders, 1)
            step(nc.vector.memset(xs[2][:, :, :, :].rearrange("p b h w -> p (b h w)"), 0.0), "x2_border")


            def gn_stats(layer, b):
                step(nc.vector.bn_stats(st[:, layer, b, :], xs[layer][:, b, :]), "stats", layer, b)

            def gn_aggr(layer, b):
                settle("stats", layer, b)
                step(nc.vector.bn_aggr(mv[:, layer, b, 0:2], st[:, layer, b, :]), "aggr", layer, b)

            def gn_mean_sq(layer, b):
                settle("aggr", layer, b)
                nc.vector.scalar_tensor_tensor(
                    out=mv[:, layer, b, 2:3], in0=mv[:, layer, b, 0:1], scalar=mv[:, layer, b, 0:1],
                    in1=mv[:, layer, b, 1:2], op0=ALU.mult, op1=ALU.add).then_inc(stats_ready[layer], 1)

            def group_out(layer, b):
                dve.wait_ge(group_ready[layer], b + 1)
                nc.vector.tensor_tensor(gs[:, layer, b, :], gn_ps[:, 0:2], eps_row[:, :],
                                        ALU.add).then_inc(group_read[layer], 1)

            def group_var(layer, b):
                dve.wait_ge(group_read[layer], b + 1)
                g = gs[:, layer, b, :]
                nc.vector.scalar_tensor_tensor(
                    out=ve[:, layer, b:b + 1], in0=g[:, 0:1], scalar=g[:, 0:1], in1=g[:, 1:2],
                    op0=ALU.mult, op1=ALU.subtract, reverse1=True).then_inc(var_ready[layer], 1)

            def normalise(layer, b, dst, roots_done):
                dve.wait_ge(rstd_ready[layer], roots_done)
                nc.vector.tensor_scalar(dst, xs[layer][:, b, :], gs[:, layer, b, 0:1],
                                        rstd[:, layer, b:b + 1],
                                        ALU.subtract, ALU.mult).then_inc(t_ready[layer], 1)

            dve.wait_ge(x_in[0], 16)
            gn_stats(0, 0)
            gn_aggr(0, 0)
            gn_mean_sq(0, 0)
            dve.wait_ge(x_in[1], 16)
            gn_stats(0, 1)
            dve.wait_ge(pool_consts, 1)
            group_out(0, 0)
            gn_stats(0, 2)
            group_var(0, 0)
            gn_stats(0, 3)
            for b in range(1, B):
                gn_aggr(0, b)
            normalise(0, 0, t0[:, 0, :], 1)
            settle("aggr", 0, B - 1)
            step(nc.vector.tensor_tensor(msq0[:, 1:B], mv[:, 0, 1:B, 0], mv[:, 0, 1:B, 0], ALU.mult),
                 "msq0")
            settle("msq0")
            nc.vector.tensor_tensor(mv[:, 0, 1:B, 2], mv[:, 0, 1:B, 1], msq0[:, 1:B],
                                    ALU.add).then_inc(stats_ready[0], 1)
            def other_group_vars():
                dve.wait_ge(group_ready[0], 2)
                nc.vector.tensor_tensor(
                    gs[:, 0, 1:B, :], gn_ps[:, 0:2 * (B - 1)].rearrange("p (b f) -> p b f", f=2),
                    eps_row[:, :].unsqueeze(1).to_broadcast([C, B - 1, 2]),
                    ALU.add).then_inc(group_read[0], 1)
                dve.wait_ge(group_read[0], 2)
                step(nc.vector.tensor_tensor(msq0[:, 1:B], gs[:, 0, 1:B, 0], gs[:, 0, 1:B, 0], ALU.mult),
                     "gm_sq")
                settle("gm_sq")
                nc.vector.tensor_tensor(ve[:, 0, 1:B], gs[:, 0, 1:B, 1], msq0[:, 1:B],
                                        ALU.subtract).then_inc(var_ready[0], 1)

            w_out = lp[:, LC["conv_out"]]

            def sw_stats():
                dve.wait_ge(late_in, 16)
                step(nc.vector.bn_stats(sw_st[:, :], w_out), "sw_st")
                step(nc.vector.tensor_scalar(one_minus_a[:, :], lp[:, LC["prelu"]], -1.0, 1.0,
                                             ALU.mult, ALU.add), "one_minus_a")

            def sw_aggr():
                settle("sw_st")
                step(nc.vector.bn_aggr(sw_mv[:, :], sw_st[:, :]), "sw_mv")

            def sw_variance():
                settle("sw_mv")
                nc.vector.tensor_scalar(sw_var[:, :], sw_mv[:, 1:2], CONV_FAN / (CONV_FAN - 1.0),
                                        None, ALU.mult).then_inc(sw_var_ready, 1)
                step(nc.vector.tensor_scalar(sw_dev[:, :], w_out, sw_mv[:, 0:1], None, ALU.subtract),
                     "sw_dev")

            def sw_abs_sum():
                settle("sw_dev")
                step(nc.vector.tensor_reduce(sw_abs[:, :], sw_dev[:, :], X_AXIS, ALU.add,
                                             apply_absolute_value=True), "sw_abs")

            def sw_scale():
                dve.wait_ge(sw_rstd_ready, 1)
                settle("sw_abs")
                step(nc.vector.tensor_scalar(sw[:, :], sw_abs[:, :], 1.0 / CONV_FAN, sw_rstd[:, :],
                                             ALU.mult, ALU.mult), "sw")

            def sw_products():
                settle("sw")
                step(nc.vector.tensor_tensor(sw_sq[:, :], sw[:, :], sw[:, :], ALU.mult), "sw_sq")
                step(nc.vector.tensor_tensor(sw_gamma[:, :], sw[:, :], lp[:, LC["bn2_gamma"]],
                                             ALU.mult), "sw_gamma")

            def norm0(b):
                normalise(0, b, t0[:, b, :], 2)


            def k_out(b):
                dve.wait_ge(k_mm, b + 1)
                nc.vector.tensor_scalar(k[:, b, :], k_ps, ep[:, EC["bk"]], None,
                                        ALU.add).then_inc(k_ready, 1)

            def row_max(b):
                dve.wait_ge(s_mm, b + 1)
                nc.vector.tensor_reduce(nmax[:, b, :],
                                        s_ps[b % 2][:, :].rearrange("p (a c) -> p a c", a=2),
                                        X_AXIS, ALU.max, negate=True).then_inc(nmax_ready, 1)

            def rinv_out(b):
                dve.wait_ge(exp_ready, 2 * b + 2)
                step(nc.vector.reciprocal(rinv[:, b, :], psum_rows[:, b, :]), "rinv", b)

            def x1_out(b):
                dve.wait_ge(o_mm, b + 1)
                dve.wait_ge(xb_ready, b + 1)
                settle("rinv", b)
                for par in range(2):
                    side = slice(par * HALF, (par + 1) * HALF)
                    nc.vector.scalar_tensor_tensor(
                        out=xs[1][:, b, side], in0=o_ps[b][:, side], scalar=rinv[:, b, par:par + 1],
                        in1=xb[:, b, side], op0=ALU.mult, op1=ALU.add).then_inc(x1_ready, 1)

            def x1_stats(b):
                dve.wait_ge(x1_ready, 2 * b + 2)
                gn_stats(1, b)

            def norm1(b):
                normalise(1, b, res[:, b, :], b + 1)


            def bn1_mean_sq():
                dve.wait_ge(group_read[1], B)
                step(nc.vector.tensor_tensor(bn1_dev[:, :], mv[:, 1, :, 0], gs[:, 1, :, 0], ALU.subtract),
                     "bn1_dev")
                dve.wait_ge(var_ready[1], B)
                step(nc.vector.reciprocal(bn1_inv[:, :], ve[:, 1, :]), "bn1_inv")
                settle("bn1_dev")
                step(nc.vector.tensor_tensor(bn1_dev_sq[:, :], bn1_dev[:, :], bn1_dev[:, :], ALU.mult),
                     "bn1_dev_sq")
                settle("bn1_dev_sq")
                step(nc.vector.tensor_tensor(bn1_sq[:, :], bn1_dev_sq[:, :], mv[:, 1, :, 1], ALU.add),
                     "bn1_sq")
                settle("bn1_sq")
                step(nc.vector.scalar_tensor_tensor(
                    out=bn1_tmp[:, 0, :], in0=bn1_sq[:, :], scalar=1.0 / B, in1=bn1_inv[:, :],
                    op0=ALU.mult, op1=ALU.mult, accum_out=bn1_e2[:, 0:1]), "bn1_e2")

            def bn1_mean():
                dve.wait_ge(rstd_ready[1], B)
                step(nc.vector.scalar_tensor_tensor(
                    out=bn1_tmp[:, 1, :], in0=bn1_dev[:, :], scalar=1.0 / B, in1=rstd[:, 1, :],
                    op0=ALU.mult, op1=ALU.mult, accum_out=bn_mv[:, 0, 0:1]), "bn_mv", 0)
                settle("bn1_e2")
                step(nc.vector.tensor_scalar(bn1_e2[:, 1:2], bn1_e2[:, 0:1], EPS, None, ALU.add),
                     "bn1_e2_eps")

            def bn1_var():
                settle("bn1_e2_eps")
                mean = bn_mv[:, 0, 0:1]
                nc.vector.scalar_tensor_tensor(
                    out=bn_ve[:, 0:1], in0=mean, scalar=mean, in1=bn1_e2[:, 1:2], op0=ALU.mult,
                    op1=ALU.subtract, reverse1=True).then_inc(bn_var_ready, 1)

            def bn_scale_out(i):
                dve.wait_ge(bn_rstd_ready, i + 1)
                if i == 1:
                    settle("sw_gamma")
                gamma = (lp[:, LC["bn1_gamma"]], sw_gamma[:, :])[i]
                step(nc.vector.tensor_tensor(bn_scale[:, i:i + 1], bn_rs[:, i:i + 1], gamma, ALU.mult),
                     "bn_scale", i)

            def bn_shift_out(i):
                settle("bn_scale", i)
                beta = lp[:, LC[("bn1_beta", "bn2_beta")[i]]]
                nc.vector.scalar_tensor_tensor(
                    out=bn_shift[:, i:i + 1], in0=bn_mv[:, i, 0:1], scalar=bn_scale[:, i:i + 1],
                    in1=beta, op0=ALU.mult, op1=ALU.subtract, reverse1=True).then_inc(bn_shift_ready, 1)

            def bn2_stats(b):
                dve.wait_ge(conv_mm, b + 1)
                nc.vector.bn_stats(bn2_st[:, b, :], conv_ps[b]).then_inc(bn2_st_ready, 1)

            def bn2_aggr():
                dve.wait_ge(bn2_st_ready, B)
                step(nc.vector.bn_aggr(bn_mv[:, 1, :], bn2_st[:, :, :].rearrange("p b f -> p (b f)")),
                     "bn_mv", 1)

            def bn2_var():
                settle("bn_mv", 1)
                settle("sw_sq")
                nc.vector.tensor_scalar(bn_ve[:, 1:2], bn_mv[:, 1, 1:2], sw_sq[:, :], EPS,
                                        ALU.mult, ALU.add).then_inc(bn_var_ready, 1)

            def h1_out(b):
                dve.wait_ge(bn2_out_ready, b + 1)
                nc.vector.tensor_tensor(h1[:, b, :], bn2_out[:, b, :], res[:, b, :],
                                        ALU.add).then_inc(h1_ready, 1)

            def x2_out(b):
                dve.wait_ge(h1_neg_ready, b + 1)
                dve.wait_ge(x1_h1_ready, b + 1)
                if b == 0:
                    settle("x2_border")
                nc.vector.scalar_tensor_tensor(
                    out=x2_inside[:, b], in0=square(h1_neg[:, b, :]), scalar=one_minus_a[:, :],
                    in1=square(x1_h1[:, b, :]), op0=ALU.mult, op1=ALU.add,
                    accum_out=mv[:, 2, b, 0:1]).then_inc(x2_ready, 1)


            def dw_tap(b, i):
                tap = PE_TAPS + ACT_TAPS + i
                dy, dx = tap // 3, tap % 3
                if i == 0:
                    dve.wait_ge(act_sum_ready, b + 1)
                    before = act_sum[:, b, :]
                else:
                    settle("tap", b, i - 1)
                    before = dw_acc[:, b, i - 1, :]
                ins = nc.vector.scalar_tensor_tensor(
                    out=square(dw_acc[:, b, i, :]), in0=xs[2][:, b, dy:dy + H, dx:dx + W],
                    scalar=lp[:, LC["dw"].start + tap:LC["dw"].start + tap + 1],
                    in1=square(before), op0=ALU.mult, op1=ALU.add)
                if i < DVE_TAPS - 1:
                    step(ins, "tap", b, i)
                else:
                    ins.then_inc(dw_acc_ready, 1)

            def dw_merge(b):
                dve.wait_ge(dw_rest_ready, b + 1)
                dve.wait_ge(dw_mm, b + 1)
                nc.vector.tensor_tensor(dw_sum[:, b, :], dw_ps[b], dw_rest[:, b, :],
                                        ALU.add).then_inc(dw_sum_ready, 1)

            def prune1_max(b):
                dve.wait_ge(h2_ready, b + 1)
                step(nc.vector.tensor_reduce(amax[:, b, 0:1], h2[:, b, :], X_AXIS, ALU.max),
                     "amax", 0, b)

            def prune1_weights(b):
                settle("amax", 0, b)
                nc.vector.scalar_tensor_tensor(
                    out=pwT_kept[:, b, :], in0=amax[:, b, 0:1].to_broadcast([C, C]),
                    scalar=DW_THRESH, in1=lp[:, LC["pwT"]], op0=ALU.is_ge,
                    op1=ALU.mult).then_inc(pwT_ready, 1)

            def prune2_max(b):
                dve.wait_ge(y2_ready, b + 1)
                step(nc.vector.tensor_reduce(amax[:, b, 1:2], y2[:, b, :], X_AXIS, ALU.max),
                     "amax", 1, b)

            def prune2_keep(b):
                settle("amax", 1, b)
                step(nc.vector.tensor_scalar(keep[:, b:b + 1], amax[:, b, 1:2], PW_THRESH, None,
                                             ALU.is_ge), "keep", b)

            def x3_out(b):
                settle("keep", b)
                nc.vector.scalar_tensor_tensor(
                    out=square(xs[3][:, b, :]), in0=square(y2[:, b, :]), scalar=keep[:, b:b + 1],
                    in1=x2_inside[:, b], op0=ALU.mult, op1=ALU.add,
                    accum_out=mv[:, 3, b, 0:1]).then_inc(x3_ready, 1)


            def norm3(b):
                normalise(3, b, t3[:, b, :], b + 1)

            def k3_max(b):
                dve.wait_ge(k3_mm, b + 1)
                nc.vector.tensor_reduce(nmax3[:, b:b + 1], k3_ps[b], X_AXIS, ALU.max,
                                        negate=True).then_inc(nmax3_ready, 1)

            def rinv3_out(b):
                dve.wait_ge(e3_ready, b + 1)
                nc.vector.reciprocal(rinv3[:, b:b + 1], sum3[:, b:b + 1]).then_inc(rinv3_ready, 1)

            def context_out(b):
                dve.wait_ge(cx_mm, b + 1)
                if b == 0:
                    dve.wait_ge(head_mask_ready, 1)
                nc.vector.tensor_tensor(ctxT[:, b, :], cx_ps, head_mask[:, :],
                                        ALU.mult).then_inc(cx_ready, 1)

            def x4_out(b):
                dve.wait_ge(y3_mm, b + 1)
                nc.vector.scalar_tensor_tensor(out=xs[4][:, b, :], in0=y_ps,
                                               scalar=lp[:, LC["b_out"]], in1=xs[3][:, b, :],
                                               op0=ALU.add, op1=ALU.add).then_inc(x4_ready, 1)

            sw_stats()
            sw_aggr()
            other_group_vars()
            sw_variance()
            k_out(0)
            sw_abs_sum()
            norm0(1)
            norm0(2)
            norm0(3)
            row_max(0)
            k_out(1)
            rinv_out(0)
            k_out(2)
            row_max(1)
            k_out(3)
            row_max(2)
            rinv_out(1)
            row_max(3)
            rinv_out(2)
            x1_out(0)
            x1_stats(0)
            sw_scale()
            gn_aggr(1, 0)
            gn_mean_sq(1, 0)
            sw_products()
            rinv_out(3)
            x1_out(1)
            group_out(1, 0)
            group_var(1, 0)
            x1_stats(1)
            gn_aggr(1, 1)
            gn_mean_sq(1, 1)
            norm1(0)
            x1_out(2)
            group_out(1, 1)
            x1_stats(2)
            group_var(1, 1)
            gn_aggr(1, 2)
            x1_out(3)
            gn_mean_sq(1, 2)
            x1_stats(3)
            gn_aggr(1, 3)
            group_out(1, 2)
            gn_mean_sq(1, 3)
            group_var(1, 2)
            group_out(1, 3)
            group_var(1, 3)
            norm1(1)
            bn1_mean_sq()
            bn1_mean()
            bn1_var()
            norm1(2)
            norm1(3)
            bn_scale_out(0)
            bn_shift_out(0)
            bn2_stats(0)
            bn2_stats(1)
            bn2_stats(2)
            bn2_stats(3)
            bn2_aggr()
            bn2_var()
            bn_scale_out(1)
            bn_shift_out(1)
            h1_out(0)
            h1_out(1)
            h1_out(2)
            x2_out(0)
            x2_out(1)
            x2_out(2)
            h1_out(3)
            group_out(2, 0)
            group_var(2, 0)
            dw_tap(0, 0)
            x2_out(3)
            dw_tap(0, 1)
            dw_tap(1, 0)
            dw_tap(1, 1)
            group_out(2, 1)
            dw_merge(0)
            group_var(2, 1)
            group_out(2, 2)
            dw_tap(2, 0)
            group_var(2, 2)
            dw_tap(2, 1)
            dw_merge(1)
            prune1_max(0)
            prune1_weights(0)
            dw_tap(3, 0)
            group_out(2, 3)
            dw_tap(3, 1)
            dw_merge(2)
            prune1_max(1)
            prune2_max(0)
            group_var(2, 3)
            prune2_keep(0)
            prune1_weights(1)
            x3_out(0)
            prune1_max(2)
            dw_merge(3)
            prune1_weights(2)
            prune2_max(1)
            group_out(3, 0)
            prune2_keep(1)
            group_var(3, 0)
            x3_out(1)
            prune1_max(3)
            prune2_max(2)
            prune1_weights(3)
            norm3(0)
            group_out(3, 1)
            prune2_keep(2)
            group_var(3, 1)
            x3_out(2)
            k3_max(0)
            prune2_max(3)
            norm3(1)
            group_out(3, 2)
            prune2_keep(3)
            group_var(3, 2)
            rinv3_out(0)
            x3_out(3)
            k3_max(1)
            norm3(2)
            rinv3_out(1)
            group_out(3, 3)
            group_var(3, 3)
            k3_max(2)
            context_out(0)
            norm3(3)
            rinv3_out(2)
            k3_max(3)
            context_out(1)
            x4_out(0)
            rinv3_out(3)
            context_out(2)
            x4_out(1)
            context_out(3)
            x4_out(2)
            x4_out(3)
        @block.tensor
        def _(pe):
            def keep_warm(count, bank=warm_ps):
                for _ in range(count):
                    nc.tensor.matmul(bank[:, 0:N], warm[:, 0:C], warm[:, :],
                                     start=True, stop=True)

            last_in_bank7 = []

            def take_bank7(read, count):
                if last_in_bank7:
                    pe.wait_ge(*last_in_bank7.pop())
                last_in_bank7.append((read, count))

            def group_means(layer, b):
                if layer == 2 and b == 0:
                    pe.wait_ge(sum_masks, 1)
                pe.wait_ge(stats_ready[layer], b + 1)
                take_bank7(group_read[layer], b + 1)
                nc.tensor.matmul(gn_ps[:, 0:2], (group_avg if layer < 2 else group_sum)[:, :],
                                 mv[:, layer, b, 0:3:2],
                                 start=True, stop=True).then_inc(group_ready[layer], 1)

            def fold_weights():
                pe.wait_ge(early_in, 16)
                nc.tensor.matmul(setup_ps[:, 0:C], ep[:, EC["wv"]], ep[:, EC["woT"]],
                                 start=True, stop=True)

            def fold_bias():
                pe.wait_ge(pool_consts, 2)
                nc.tensor.matmul(setup_ps[:, C:2 * C], bias_rows[:, 0, :], ep[:, EC["woT"]],
                                 start=True, stop=False)
                nc.tensor.matmul(setup_ps[:, C:2 * C], bias_rows[:, 1, :], ident[:, :],
                                 start=False, stop=True).then_inc(setup_mm, 1)


            def other_group_means():
                pe.wait_ge(stats_ready[0], 2)
                take_bank7(group_read[0], 2)
                nc.tensor.matmul(gn_ps[:, 0:2 * (B - 1)].rearrange("p (b f) -> p b f", f=2),
                                 group_avg[:, :], mv[:, 0, 1:B, 0:3:2],
                                 start=True, stop=True).then_inc(group_ready[0], 1)

            def project_q(b):
                pe.wait_ge(t_ready[0], b + 1)
                if b >= 1:
                    pe.wait_ge(q_ready, b)
                nc.tensor.matmul(q_ps, ep[:, EC["wqT"]], t0[:, b, :],
                                 start=True, stop=True).then_inc(q_mm, 1)

            def project_k(b):
                pe.wait_ge(t_ready[0], b + 1)
                if b >= 1:
                    pe.wait_ge(k_ready, b)
                nc.tensor.matmul(k_ps, ep[:, EC["wkT"]], t0[:, b, :],
                                 start=True, stop=True).then_inc(k_mm, 1)

            def project_v(b):
                pe.wait_ge(t_ready[0], b + 1)
                if b == 0:
                    pe.wait_ge(setup_done, 2)
                else:
                    pe.wait_ge(v_ready, b)
                for j in range(2):
                    ins = nc.tensor.matmul(v_ps[:, j * C:(j + 1) * C],
                                           t0[:, b, j * C:(j + 1) * C], woT_v,
                                           start=True, stop=True)
                ins.then_inc(v_mm, 1)

            def scores(b):
                pe.wait_ge(q_ready, b + 1)
                pe.wait_ge(k_ready, b + 1)
                if b >= 2:
                    pe.wait_ge(exp_ready, 2 * (b - 1))
                for par in range(2):
                    ins = nc.tensor.matmul(s_ps[b % 2][:, par * N:(par + 1) * N], q[:, b, par:N:2],
                                           k[:, b, :], start=True, stop=True)
                ins.then_inc(s_mm, 1)

            def transpose_prob(b):
                if b >= 1:
                    pe.wait_ge(pt_ready, b)
                for par in range(2):
                    pe.wait_ge(exp_ready, 2 * b + par + 1)
                    for j in range(2):
                        at = (2 * j + par) * C
                        ins = nc.tensor.transpose(pt_ps[:, at:at + C],
                                                  prob[:, b, par, j * C:(j + 1) * C], ident[:, :])
                ins.then_inc(pt_mm, 1)

            def attend(b):
                pe.wait_ge(v_ready, b + 1)
                pe.wait_ge(pt_ready, b + 1)
                if b == 3:
                    pe.wait_ge(k_ready, B)
                elif b >= 1:
                    pe.wait_ge(x1_ready, 2 * b)
                for par in range(2):
                    for j in range(2):
                        ins = nc.tensor.matmul(o_ps[b][:, par * C:(par + 1) * C],
                                               probT[:, b, j, par, :], vt[:, b, j, :],
                                               start=(j == 0), stop=(j == 1))
                ins.then_inc(o_mm, 1)


            def conv(b):
                if b == 0:
                    pe.wait_ge(conv_w_ready, 1)
                pe.wait_ge(sign_ready, b + 1)
                for tap in range(TAPS):
                    dy, dx = tap // 3, tap % 3
                    ins = nc.tensor.matmul(conv_ps[b], conv_w[:, tap, :],
                                           signs[:, b, dy:dy + H, dx:dx + W],
                                           start=(tap == 0), stop=(tap == TAPS - 1))
                ins.then_inc(conv_mm, 1)


            def valid_taps(tap):
                if tap == 0:
                    pe.wait_ge(sum_masks, 1)
                    pe.wait_ge(exp_ready, 2 * 3)
                pe.wait_ge(dw_diag_ready, tap + 1)
                dy, dx = tap // 3, tap % 3
                ins = nc.tensor.matmul(valid_ps, dw_diag[:, tap, :], valid[:, dy:dy + H, dx:dx + W],
                                       start=(tap == 0), stop=(tap == TAPS - 1))
                if tap == TAPS - 1:
                    ins.then_inc(valid_mm, 1)

            def depthwise(b):
                pe.wait_ge(x2_ready, b + 1)
                if b == 0:
                    pe.wait_ge(valid_ready, 1)
                elif b >= 2:
                    pe.wait_ge(dw_sum_ready, b - 1)
                for tap in range(PE_TAPS):
                    dy, dx = tap // 3, tap % 3
                    ins = nc.tensor.matmul(dw_ps[b], dw_diag[:, tap, :],
                                           xs[2][:, b, dy:dy + H, dx:dx + W],
                                           start=(tap == 0), stop=(tap == PE_TAPS - 1))
                ins.then_inc(dw_mm, 1)

            def pointwise(b):
                pe.wait_ge(pwT_ready, b + 1)
                if b >= 1:
                    pe.wait_ge(y2_ready, b)
                nc.tensor.matmul(pw_ps, pwT_kept[:, b, :], h2[:, b, :],
                                 start=True, stop=True).then_inc(pw_mm, 1)

            wqkv = [lp[:, LC["wqkvT"].start + i * C:LC["wqkvT"].start + (i + 1) * C] for i in range(3)]

            def project_k3(b):
                pe.wait_ge(t_ready[3], b + 1)
                if b == 0:
                    pe.wait_ge(bn2_out_ready, B)
                elif b == 1:
                    pe.wait_ge(dw_sum_ready, B)
                else:
                    pe.wait_ge(e3_ready, b - 1)
                nc.tensor.matmul(k3_ps[b], wqkv[1], t3[:, b, :],
                                 start=True, stop=True).then_inc(k3_mm, 1)

            def project_q3(b):
                pe.wait_ge(t_ready[3], b + 1)
                if b == 0:
                    pe.wait_ge(bn2_out_ready, B)
                else:
                    pe.wait_ge(q3_ready, b)
                nc.tensor.matmul(q_ps, wqkv[0], t3[:, b, :], start=True, stop=True).then_inc(q3_mm, 1)

            def project_v3(b):
                pe.wait_ge(t_ready[3], b + 1)
                if b == 0:
                    pe.wait_ge(dw_sum_ready, 3)
                else:
                    pe.wait_ge(vt3_ready, b)
                for j in range(2):
                    ins = nc.tensor.matmul(vt_ps[:, j * C:(j + 1) * C], t3[:, b, j * C:(j + 1) * C],
                                           wqkv[2], start=True, stop=True)
                ins.then_inc(vt3_mm, 1)

            def transpose_k(b):
                if b == 0:
                    pe.wait_ge(bn2_out_ready, B)
                else:
                    pe.wait_ge(kt3_ready, b)
                pe.wait_ge(e3_ready, b + 1)
                for j in range(2):
                    ins = nc.tensor.transpose(kt_ps[:, j * C:(j + 1) * C],
                                              e3[:, b, j * C:(j + 1) * C], ident[:, :])
                ins.then_inc(kt3_mm, 1)

            def context(b):
                pe.wait_ge(kt3_ready, b + 1)
                pe.wait_ge(vt3_ready, b + 1)
                take_bank7(cx_ready, b + 1)
                for j in range(2):
                    ins = nc.tensor.matmul(cx_ps, vt3[:, b, j, :], kt3[:, b, j, :],
                                           start=(j == 0), stop=(j == 1))
                ins.then_inc(cx_mm, 1)

            def project_context(b):
                pe.wait_ge(cx_ready, b + 1)
                if b == 0:
                    pe.wait_ge(y2_ready, B)
                else:
                    pe.wait_ge(pj_ready, b)
                nc.tensor.matmul(pj_ps, ctxT[:, b, :], lp[:, LC["woutT"]],
                                 start=True, stop=True).then_inc(pj_mm, 1)

            def output(b):
                pe.wait_ge(q3_ready, b + 1)
                pe.wait_ge(pj_ready, b + 1)
                if b == 0:
                    pe.wait_ge(bn2_out_ready, B)
                else:
                    pe.wait_ge(x4_ready, b)
                nc.tensor.matmul(y_ps, proj[:, b, :], q3[:, b, :],
                                 start=True, stop=True).then_inc(y3_mm, 1)

            pe.wait_ge(warm_ready, 1)
            keep_warm(14)
            pe.wait_ge(gn_consts, 1)
            group_means(0, 0)
            keep_warm(5)
            fold_weights()
            keep_warm(2)
            other_group_means()
            project_q(0)
            project_k(0)
            fold_bias()
            scores(0)
            project_v(0)
            project_q(1)
            project_k(1)
            project_v(1)
            project_q(2)
            project_k(2)
            scores(1)
            project_q(3)
            project_k(3)
            scores(2)
            transpose_prob(0)
            scores(3)
            transpose_prob(1)
            attend(0)
            transpose_prob(2)
            project_v(2)
            attend(1)
            group_means(1, 0)
            project_v(3)
            transpose_prob(3)
            attend(2)
            group_means(1, 1)
            attend(3)
            valid_taps(0)
            valid_taps(1)
            group_means(1, 2)
            valid_taps(2)
            group_means(1, 3)
            valid_taps(3)
            valid_taps(4)
            valid_taps(5)
            valid_taps(6)
            valid_taps(7)
            valid_taps(8)
            conv(0)
            conv(1)
            conv(2)
            conv(3)
            keep_warm(33)
            depthwise(0)
            group_means(2, 0)
            depthwise(1)
            group_means(2, 1)
            group_means(2, 2)
            depthwise(2)
            group_means(2, 3)
            pointwise(0)
            depthwise(3)
            pointwise(1)
            keep_warm(3, y_ps)
            group_means(3, 0)
            pointwise(2)
            keep_warm(10, y_ps)
            group_means(3, 1)
            pointwise(3)
            project_k3(0)
            project_v3(0)
            project_q3(0)
            group_means(3, 2)
            project_k3(1)
            project_v3(1)
            project_q3(1)
            transpose_k(0)
            group_means(3, 3)
            project_k3(2)
            transpose_k(1)
            context(0)
            project_q3(2)
            project_v3(2)
            project_context(0)
            project_k3(3)
            context(1)
            output(0)
            transpose_k(2)
            project_context(1)
            project_v3(3)
            context(2)
            transpose_k(3)
            output(1)
            project_context(2)
            context(3)
            project_q3(3)
            output(2)
            project_context(3)
            output(3)


def kernel(**inputs):
    import numpy as np
    import concourse.bacc as bacc
    from concourse.bass_utils import run_bass_kernel_spmd

    def arr(name):
        return np.ascontiguousarray(np.asarray(inputs[name]))

    def col(*names):
        return np.stack([arr(n) for n in names], axis=1)

    conv = arr("L1_conv_conv_w").reshape(C // CONV_GROUP, CONV_GROUP, CONV_GROUP, TAPS)
    early = [arr("L0_conv_Wq").T, arr("L0_conv_Wk").T, arr("L0_conv_Wv"), arr("L0_conv_Wo").T,
             col("L0_conv_bq", "L0_conv_bk", "L0_conv_bv", "L0_conv_bo")]
    late = [conv.transpose(0, 2, 3, 1).reshape(C, TAPS * CONV_GROUP),
            arr("L1_conv_conv_w").reshape(C, CONV_FAN), arr("L2_conv_dw_w").reshape(C, TAPS),
            col("L1_conv_bn1_gamma", "L1_conv_bn1_beta", "L1_conv_bn2_gamma", "L1_conv_bn2_beta",
                "L1_conv_prelu_a", "L2_conv_dw_b", "L2_conv_pw_b", "L2_conv_bn1_g", "L2_conv_bn2_g",
                "L2_conv_bn1_b", "L2_conv_bn2_b", "L2_conv_bn1_m", "L2_conv_bn2_m", "L2_conv_bn1_v",
                "L2_conv_bn2_v", "L3_conv_b_out"),
            arr("L2_conv_pw_w").reshape(C, C).T, arr("L3_conv_w_qkv").T, arr("L3_conv_w_out").T]
    arrays = {"x": arr("x"), "early": np.ascontiguousarray(np.concatenate(early, axis=1)),
              "late": np.ascontiguousarray(np.concatenate(late, axis=1))}

    nc = bacc.Bacc("TRN2", target_bir_lowering=False, num_devices=1)
    args = [nc.dram_tensor(f"in_{name}", a.shape, mybir.dt.float32, kind="ExternalInput").ap()
            for name, a in arrays.items()]
    out = nc.dram_tensor("out", (B, C, H, W), mybir.dt.float32, kind="ExternalOutput").ap()
    build(nc, *args, out)
    r = run_bass_kernel_spmd(nc, [{f"in_{name}": a for name, a in arrays.items()}], core_ids=[0])
    return r.results[0]["out"]
```
